# Optimizing a Trainium2 kernel written in Bass

```python
import numpy as np
import jax
import jax.numpy as jnp

def _softmax(x, axis=-1):
    return jax.nn.softmax(x, axis=axis)

def _gelu(x):
    return jax.nn.gelu(x, approximate=True)

def _silu(x):
    return jax.nn.silu(x)

def _sigmoid(x):
    return jax.nn.sigmoid(x)

def _layernorm(x, axis=-1, eps=1e-05):
    m = jnp.mean(x, axis=axis, keepdims=True)
    v = jnp.var(x, axis=axis, keepdims=True)
    return (x - m) / jnp.sqrt(v + eps)

def _scatter_add(tgt, idx, src, axis=0):
    return tgt.at[idx].add(src)

def _segment_sum(src, seg, n):
    return jax.ops.segment_sum(src, seg, n)
kernel_name = 'mk_adaln_d1_jaxref_r8_32c2e7'

def setup_inputs(seed: int=0):
    np.random.seed(seed)
    _w = jnp.asarray

    def _L0_attn_setup():
        import jax, jax.numpy as jnp
        import numpy as np
        EMBED_DIM = 256
        NUM_HEADS = 16
        HEAD_DIM = EMBED_DIM // NUM_HEADS
        D_K = 128
        SCALE = 1.0 / float(np.sqrt(HEAD_DIM))
        LAYER_DEPTH = 6 / 12
        BATCH, SEQ = (2, 256)
        key = jax.random.key(seed)
        ks = jax.random.split(key, 8)
        return {'hidden_states': jax.random.normal(ks[0], (BATCH, SEQ, EMBED_DIM), jnp.float32), 'c_attn_w': jax.random.normal(ks[1], (EMBED_DIM, 3 * EMBED_DIM), jnp.float32) * 0.02, 'c_attn_b': jax.random.normal(ks[2], (3 * EMBED_DIM,), jnp.float32) * 0.02, 'c_proj_w': jax.random.normal(ks[3], (EMBED_DIM, EMBED_DIM), jnp.float32) * 0.02, 'c_proj_b': jax.random.normal(ks[4], (EMBED_DIM,), jnp.float32) * 0.02, 'cam_gate': jax.random.normal(ks[5], (D_K,), jnp.float32) * 0.1, 'cam_w0': jax.random.normal(ks[6], (1,), jnp.float32), 'cam_w1': jax.random.normal(ks[7], (1,), jnp.float32)}
    _L0_attn_in = _L0_attn_setup()

    def _L0_ffn_setup():
        import jax, jax.numpy as jnp
        import numpy as np
        L, N, E, H, K = (256, 8, 256, 1024, 8)
        key = jax.random.key(seed)
        ks = jax.random.split(key, 6)
        return {'x': jax.random.normal(ks[0], (L, N, E), dtype=jnp.float32), 'proj1': jax.random.normal(ks[1], (H, E), dtype=jnp.float32) * 0.02, 'proj1_bias': jax.random.normal(ks[2], (H,), dtype=jnp.float32) * 0.02, 'proj2': jax.random.normal(ks[3], (E, H), dtype=jnp.float32) * 0.02, 'proj2_bias': jax.random.normal(ks[4], (E,), dtype=jnp.float32) * 0.02, 'gate_w': jax.random.normal(ks[5], (E, K), dtype=jnp.float32)}
    _L0_ffn_in = _L0_ffn_setup()
    _L0_c = _w((lambda *s: np.random.randn(*s).astype(np.float32) * 0.05)(2, 256))
    _L0_wmod = _w((lambda *s: np.random.randn(*s).astype(np.float32) * 0.05)(256, 6 * 256) * 256 ** (-0.5))
    _d = {'L0_attn_hidden_states': _L0_attn_in['hidden_states'], 'L0_attn_c_attn_w': _L0_attn_in['c_attn_w'], 'L0_attn_c_attn_b': _L0_attn_in['c_attn_b'], 'L0_attn_c_proj_w': _L0_attn_in['c_proj_w'], 'L0_attn_c_proj_b': _L0_attn_in['c_proj_b'], 'L0_attn_cam_gate': _L0_attn_in['cam_gate'], 'L0_attn_cam_w0': _L0_attn_in['cam_w0'], 'L0_attn_cam_w1': _L0_attn_in['cam_w1'], 'L0_ffn_proj1': _L0_ffn_in['proj1'], 'L0_ffn_proj1_bias': _L0_ffn_in['proj1_bias'], 'L0_ffn_proj2': _L0_ffn_in['proj2'], 'L0_ffn_proj2_bias': _L0_ffn_in['proj2_bias'], 'L0_ffn_gate_w': _L0_ffn_in['gate_w'], 'L0_c': _L0_c, 'L0_wmod': _L0_wmod}
    _x0 = _d['L0_attn_hidden_states']
    _d['L0_attn_hidden_states'] = jax.random.normal(jax.random.fold_in(jax.random.key(seed), 1), (2, 1024, 256), dtype=_x0.dtype)
    del _x0
    return _d

def reference(L0_attn_hidden_states, L0_attn_c_attn_w, L0_attn_c_attn_b, L0_attn_c_proj_w, L0_attn_c_proj_b, L0_attn_cam_gate, L0_attn_cam_w0, L0_attn_cam_w1, L0_ffn_proj1, L0_ffn_proj1_bias, L0_ffn_proj2, L0_ffn_proj2_bias, L0_ffn_gate_w, L0_c, L0_wmod):

    def _L0_attn_ref(hidden_states, c_attn_w, c_attn_b, c_proj_w, c_proj_b, cam_gate, cam_w0, cam_w1):
        import jax, jax.numpy as jnp
        import numpy as np
        EMBED_DIM = 256
        NUM_HEADS = 16
        HEAD_DIM = EMBED_DIM // NUM_HEADS
        D_K = 128
        SCALE = 1.0 / float(np.sqrt(HEAD_DIM))
        LAYER_DEPTH = 6 / 12
        BATCH, SEQ = (2, 256)
        qkv = hidden_states @ c_attn_w + c_attn_b
        Q, K, V = jnp.split(qkv, 3, axis=2)
        attn_scores = jnp.einsum('bse,bte->bst', Q, K) * SCALE
        Q_cam, K_cam, V_cam = (Q[:, :, :D_K], K[:, :, :D_K], V[:, :, :D_K])
        base_A = jax.lax.stop_gradient(jax.nn.softmax(jnp.einsum('bsd,btd->bst', Q_cam, K_cam) * SCALE, axis=-1))
        layer_weight = jax.nn.sigmoid(cam_w0[0] + cam_w1[0] * LAYER_DEPTH)
        cam_ctx = jnp.einsum('bst,btd->bsd', base_A, V_cam)
        cam_bias = jnp.einsum('bsd,btd->bst', jnp.tanh(cam_ctx * cam_gate), K_cam)
        cam_bias = cam_bias * (SCALE * layer_weight)
        final_attn = jax.nn.softmax(attn_scores + cam_bias, axis=-1)
        context = jnp.einsum('bst,bte->bse', final_attn, V)
        output = context @ c_proj_w + c_proj_b
        return output

    def _L0_ffn_ref(x, proj1, proj1_bias, proj2, proj2_bias, gate_w):
        import jax, jax.numpy as jnp
        import numpy as np
        L, N, E, H, K = (256, 8, 256, 1024, 8)
        dst = jnp.argmax(jnp.einsum('lne,ek->lnk', x, gate_w), axis=-1)
        h = jax.nn.gelu(jnp.einsum('lne,he->lnh', x, proj1) + proj1_bias, approximate=False)
        out = jnp.einsum('lnh,eh->lne', h, proj2) + proj2_bias
        del dst
        return out
    x = L0_attn_hidden_states
    mod = (_silu(L0_c) @ L0_wmod).reshape(L0_c.shape[0], 6, 1, -1)
    sa, ca, ga, sb, cb, gb = (mod[:, 0], mod[:, 1], mod[:, 2], mod[:, 3], mod[:, 4], mod[:, 5])
    ga = (2 * (ga >= 0) - 1) * jnp.maximum(jnp.abs(ga), 0.25)
    gb = (2 * (gb >= 0) - 1) * jnp.maximum(jnp.abs(gb), 0.25)
    h = _layernorm(x, axis=-1) * (1 + ca) + sa
    x = x + ga * _L0_attn_ref(h, L0_attn_c_attn_w, L0_attn_c_attn_b, L0_attn_c_proj_w, L0_attn_c_proj_b, L0_attn_cam_gate, L0_attn_cam_w0, L0_attn_cam_w1)
    h = _layernorm(x, axis=-1) * (1 + cb) + sb
    x = x + gb * _L0_ffn_ref(h, L0_ffn_proj1, L0_ffn_proj1_bias, L0_ffn_proj2, L0_ffn_proj2_bias, L0_ffn_gate_w)
    return x

_drawn_inputs = setup_inputs


def setup_inputs(seed=0):
    import zlib

    import numpy as np

    out = dict(_drawn_inputs(seed))
    spreads = {}
    factors = {'L0_attn_c_attn_w': 8.0,
     'L0_attn_c_attn_b': 8.0,
     'L0_attn_c_proj_w': 8.0,
     'L0_attn_c_proj_b': 21.408,
     'L0_attn_cam_gate': 8.0,
     'L0_ffn_proj1_bias': 57.953,
     'L0_ffn_proj2_bias': 21.4,
     'L0_ffn_proj1': 3.682,
     'L0_ffn_proj2': 3.164}
    for name, (base, spread) in spreads.items():
        noise = np.random.default_rng([zlib.crc32(name.encode()), seed]).standard_normal(out[name].shape)
        drawn = base * np.exp(spread * noise) if base else spread * noise
        out[name] = jnp.asarray(drawn.astype(out[name].dtype))
    for name, factor in factors.items():
        out[name] = (out[name] * factor).astype(out[name].dtype)
    return out
```

```python
import concourse.bass as bass
from concourse import mybir
from contextlib import ExitStack

F32 = mybir.dt.float32
F32R = mybir.dt.float32r
ACT = mybir.ActivationFunctionType
ALU = mybir.AluOpType
AX = mybir.AxisListType

P = 128
B, S, E, H = 2, 1024, 256, 1024
DK = 128
EC, HC = E // P, H // P
T = S // P
HALF = 512
TH = HALF // P
QSCALE = 0.25
EPS = 1e-5
DEPTH = 0.5
NV = DK + E
UNITS = 2 * T

C_CT, C_BQ, C_BK, C_BVC, C_BV, C_GATE, C_B1, C_W0, C_W1 = 0, 4, 6, 8, 9, 11, 12, 20, 21
NCOLS = 22


def adaln_block_kernel(nc, x, cols, wmod, w_attn, wv_t, wp, rows, w1_t, w2_t, out):
    x_v = x.rearrange("b (t p) e -> p (b t) e", p=P)
    out_v = out.rearrange("b (t p) e -> p (b t) e", p=P)

    ctx = ExitStack()
    raw = ExitStack()
    with ctx:
        def sb(name, shape, dt=F32, scope=ctx):
            return scope.enter_context(nc.sbuf_tensor(name, shape, dt))

        def sem(name):
            return ctx.enter_context(nc.semaphore(name))

        x_all = sb("x_all", [P, B * T, E])
        ident = sb("ident", [P, P])
        cols_sb = sb("cols_sb", [P, NCOLS])
        small = sb("small", [P, 32])
        modc = sb("modc", [P, B, 8])
        modb = sb("modb", [P, 8])
        gates = sb("gates", [P, B, 2, E])
        consts = sb("consts", [P, B, 2, E])
        wqk_hi, wqk_lo = (sb(f"wqk_{n}", [P, EC, 2 * E], F32R) for n in ("hi", "lo"))
        wv_hi, wv_lo = (sb(f"wv_{n}", [P, EC, NV], F32R) for n in ("hi", "lo"))
        w1_hi, w1_lo = (sb(f"w1_{n}", [P, EC, H], F32R) for n in ("hi", "lo"))
        w2_hi, w2_lo = (sb(f"w2_{n}", [P, HC, E], F32R) for n in ("hi", "lo"))
        bst = sb("bst", [P, T, 6])
        mv = sb("mv", [P, T, 2])
        ve = sb("ve", [P, T])
        rstd = sb("rstd", [P, T])
        xn = sb("xn", [P, TH, E])
        h32 = sb("h32", [P, 2, HALF])
        f32s = sb("f32s", [P, 3, HALF])
        ht_hi, ht_lo = (sb(f"ht_{n}", [P, EC, S], F32R) for n in ("hi", "lo"))
        q_hi, q_lo = (sb(f"q_{n}", [P, EC, S], F32R) for n in ("hi", "lo"))
        k_hi, k_lo = (sb(f"k_{n}", [P, EC, S], F32R) for n in ("hi", "lo"))
        v_hi, v_lo = (sb(f"v_{n}", [P, T, NV], F32R) for n in ("hi", "lo"))
        nmax = sb("nmax", [P, UNITS])
        rsum = sb("rsum", [P, UNITS])
        rinv = sb("rinv", [P, UNITS])
        th = sb("th", [P, 2, 2 * P])
        o1 = sb("o1", [P, 2, E])

        with raw:
            w1_raw = sb("w1_raw", [P, EC, H], scope=raw)
            w2_raw = sb("w2_raw", [P, HC, E], scope=raw)
            wattn_raw = sb("wattn_raw", [P, EC, 3 * E], scope=raw)
            wvt_raw = sb("wvt_raw", [P, EC, E], scope=raw)
            wp_raw = sb("wp_raw", [P, EC, E], scope=raw)
            wmod_raw = sb("wmod_raw", [P, EC, 6 * E], scope=raw)
            rows_raw = sb("rows_raw", [1, 2 * E], scope=raw)
            sct = sb("sct", [P, EC, B], scope=raw)
            scb = sb("scb", [P, EC, B, P], scope=raw)
            bvb = sb("bvb", [P, EC, P], scope=raw)
            ones_row = sb("ones_row", [1, P], scope=raw)
        pt_hi, pt_lo = (sb(f"pt_{n}", [P, 2, T, 2 * P], F32R) for n in ("hi", "lo"))
        prob = sb("prob", [P, 3, S])
        gt_hi, gt_lo = (a[:, :, :, :].rearrange("p a t n -> p (a t n)")
                        .rearrange("p (h n) -> p h n", n=HALF) for a in (pt_hi, pt_lo))

        s_ps = [ctx.enter_context(nc.psum_tensor(f"s_ps{i}", [P, 2 * HALF], F32)) for i in range(2)]
        t_ps = [ctx.enter_context(nc.psum_tensor(f"t_ps{i}", [P, HALF], F32)) for i in range(2)]
        a_ps = [ctx.enter_context(nc.psum_tensor(f"a_ps{i}", [P, HALF], F32)) for i in range(2)]

        def s_bank(k):
            return s_ps[k // 2][:, (k % 2) * HALF:(k % 2 + 1) * HALF]

        def f(ap):
            return ap.bitcast(F32)

        cols_in, wmod_in, wattn_in, wvt_in, wp_in, rows_in, w1_in, w2_in = (
            sem(n) for n in ("cols_in", "wmod_in", "wattn_in", "wvt_in", "wp_in", "rows_in", "w1_in", "w2_in"))
        x_in = [sem(f"x_in{i}") for i in range(2 * B)]
        const_ready, ident_ready, pre_act, pre_dve, silu_ready, modt_psum, gate_psum, wvp_psum, row_psum, \
            wprep_hi, wprep_lo, wffn_hi, wffn_lo = (
                sem(n) for n in ("const_ready", "ident_ready", "pre_act", "pre_dve", "silu_ready", "modt_psum",
                                 "gate_psum", "wvp_psum", "row_psum", "wprep_hi", "wprep_lo", "wffn_hi", "wffn_lo"))

        per = {}

        def lsem(name, n):
            s = sem(name)
            per[s] = n
            return s

        modb_ready = lsem("modb_ready", 1)
        bst_ready = lsem("bst_ready", 4)
        mv_ready = lsem("mv_ready", 4)
        ve_ready = lsem("ve_ready", 4)
        rstd_ready = lsem("rstd_ready", 4)
        xn_ready = lsem("xn_ready", 4)
        ht_psum = lsem("ht_psum", 8)
        h32_ready = lsem("h32_ready", 8)
        hhi_ready = lsem("hhi_ready", 8)
        hlo_ready = lsem("hlo_ready", 8)
        qk_psum = lsem("qk_psum", 8)
        qk32_ready = lsem("qk32_ready", 8)
        qkhi_ready = lsem("qkhi_ready", 8)
        qklo_ready = lsem("qklo_ready", 8)
        v_psum = lsem("v_psum", T)
        vhi_ready = lsem("vhi_ready", T)
        vlo_ready = lsem("vlo_ready", T)
        s_psum = lsem("s_psum", UNITS)
        nmax_ready = lsem("nmax_ready", UNITS)
        exp_ready = lsem("exp_ready", UNITS)
        rinv_ready = lsem("rinv_ready", UNITS)
        pnorm_ready = lsem("pnorm_ready", T)
        t_psum = lsem("t_psum", 2 * UNITS)
        pthi_ready = lsem("pthi_ready", 2 * UNITS)
        ptlo_ready = lsem("ptlo_ready", 2 * UNITS)
        ctx_psum = lsem("ctx_psum", T // 2)
        tanh_ready = lsem("tanh_ready", T // 2)
        qcam_ready = lsem("qcam_ready", T)
        qphi_ready = lsem("qphi_ready", T // 2)
        qplo_ready = lsem("qplo_ready", T // 2)
        pv_psum = lsem("pv_psum", T)
        o1_ready = lsem("o1_ready", T)
        xc_ready = lsem("xc_ready", T)
        x2_ready = lsem("x2_ready", T)
        x2c_ready = lsem("x2c_ready", T)
        f1_psum = lsem("f1_psum", 2 * HC)
        gelu_ready = lsem("gelu_ready", 2 * HC)
        ghi_ready = lsem("ghi_ready", 2 * HC)
        glo_ready = lsem("glo_ready", 2 * HC)
        f2_psum = lsem("f2_psum", T)
        t2_ready = lsem("t2_ready", T)
        y_ready = lsem("y_ready", T)
        y_out = sem("y_out")

        def wait(eng, s, it, k):
            assert 1 <= k <= per[s]
            eng.wait_ge(s, it * per[s] + k)

        def apart(eng):
            eng.wait_ge(const_ready, 2)

        def mm3(o, st_hi, st_lo, mv_hi, mv_lo, first=True, last=True):
            nc.tensor.matmul(o, st_hi, mv_hi, start=first, stop=False)
            nc.tensor.matmul(o, st_hi, mv_lo, start=False, stop=False)
            return nc.tensor.matmul(o, st_lo, mv_hi, start=False, stop=last)

        A_JOBS = ([("v", t) for t in range(T)] + [("qk", 4), ("qk", 5), ("ctx", 0), ("qk", 6), ("qk", 7), ("ctx", 1), ("ctx", 2),
                  ("ctx", 3)] + [("pv", i) for i in range(T)] + [("f2", t) for t in range(T)])
        READ_OUT = {"v": vlo_ready, "qk": qk32_ready, "ctx": tanh_ready, "pv": o1_ready, "f2": t2_ready}
        T_JOBS = ([("h", r) for r in range(4)] + [("p", n) for n in range(2 * (UNITS - 1))]
                  + [("h", 4), ("h", 5)] + [("p", 2 * UNITS - 2), ("p", 2 * UNITS - 1)] + [("h", 6), ("h", 7)])
        T_READ_OUT = {"h": h32_ready, "p": ptlo_ready}

        def a_bank(kind, k):
            return a_ps[A_JOBS.index((kind, k)) % 2]

        def t_bank(kind, k):
            return t_ps[T_JOBS.index((kind, k)) % 2]

        QK_JOBS = [(0, 0), (2, 0), (0, 1), (2, 1), (1, 0), (3, 0), (1, 1), (3, 1)]

        block = ctx.enter_context(nc.Block())

        @block.sync
        def _(sp):
            sp.dma_start(cols_sb[:, :], cols).then_inc(cols_in, 16)
            for h in range(2):
                sp.dma_start(x_all[:, h * TH:(h + 1) * TH, :], x_v[:, h * TH:(h + 1) * TH, :]).then_inc(x_in[h], 16)
                if h == 0:
                    sp.dma_start(wmod_raw[:, :, :], wmod.rearrange("(c p) n -> p c n", p=P)).then_inc(wmod_in, 16)
            for it in range(B):
                for t in range(T):
                    wait(sp, y_ready, it, t + 1)
                    sp.dma_start(out_v[:, bass.ds(it * T + t, 1), :], x_all[:, bass.ds(it * T + t, 1), :]).then_inc(y_out, 16)
            sp.wait_ge(y_out, 16 * B * T)

        @block.gpsimd
        def _(pool):
            nc.gpsimd.memset(ident[:, :], 0.0).then_inc(const_ready, 1)
            nc.gpsimd.memset(ones_row[:, :], 1.0)
            nc.gpsimd.memset(small[:, 16:24], -0.5).then_inc(const_ready, 1)
            pool.wait_ge(const_ready, 2)
            nc.gpsimd.affine_select(out=ident[:, :], in_=ident[:, :], compare_op=ALU.not_equal, fill=1.0,
                                    base=0, pattern=[[-1, P]], channel_multiplier=1).then_inc(ident_ready, 1)
            pool.wait_ge(x_in[0], 16)
            pool.dma_start(w1_raw[:, :, :], w1_t.rearrange("(c p) n -> p c n", p=P)).then_inc(w1_in, 16)
            pool.dma_start(w2_raw[:, :, :], w2_t.rearrange("(c p) n -> p c n", p=P)).then_inc(w2_in, 16)
            for h in range(2):
                a = T + h * TH
                pool.dma_start(x_all[:, a:a + TH, :], x_v[:, a:a + TH, :]).then_inc(x_in[2 + h], 16)

            def inv_std(it, n):
                h = n % 2
                wait(pool, ve_ready, it, n + 1)
                nc.gpsimd.tensor_tensor(rstd[:, h * TH:(h + 1) * TH], ve[:, h * TH:(h + 1) * TH],
                                        small[:, 16:16 + TH], ALU.pow).then_inc(rstd_ready, 1)

            def gelu_high(it, n):
                wait(pool, gelu_ready, it, n + 1)
                nc.gpsimd.tensor_scalar(gt_hi[:, n % HC, :], f32s[:, n % 3, :], 1.0, 1.0, ALU.mult, ALU.mult)\
                    .then_inc(ghi_ready, 1)

            def x2_const(it, t):
                wait(pool, xn_ready, it, 3 + t // TH)
                xt = x_all[:, bass.ds(it * T + t, 1), :]
                nc.gpsimd.tensor_tensor(xt, xt, consts[:, bass.ds(it, 1), 1, :], ALU.add).then_inc(x2c_ready, 1)

            def result(it, t):
                wait(pool, t2_ready, it, t + 1)
                wait(pool, x2c_ready, it, t + 1)
                xt = x_all[:, bass.ds(it * T + t, 1), :]
                nc.gpsimd.tensor_tensor(xt, xt, o1[:, t % 2:t % 2 + 1, :], ALU.add).then_inc(y_ready, 1)

            for n, (s, raw_w, hi, lo) in enumerate(((w1_in, w1_raw, w1_hi, w1_lo), (w2_in, w2_raw, w2_hi, w2_lo))):
                pool.wait_ge(s, 16)
                nc.gpsimd.tensor_scalar(hi[:, :, :], raw_w[:, :, :], 1.0, 1.0, ALU.mult, ALU.mult).then_inc(wffn_hi, 1)
                pool.wait_ge(wffn_hi, n + 1)
                nc.gpsimd.tensor_tensor(lo[:, :, :], raw_w[:, :, :], f(hi[:, :, :]), ALU.subtract).then_inc(wffn_lo, 1)

            def attn_const(it, t):
                wait(pool, xn_ready, it, 1 + t // TH)
                xt = x_all[:, bass.ds(it * T + t, 1), :]
                nc.gpsimd.tensor_tensor(xt, xt, consts[:, bass.ds(it, 1), 0, :], ALU.add).then_inc(xc_ready, 1)

            def attn_residual(it, t):
                wait(pool, o1_ready, it, t + 1)
                wait(pool, xc_ready, it, t + 1)
                xt = x_all[:, bass.ds(it * T + t, 1), :]
                nc.gpsimd.tensor_tensor(xt, xt, o1[:, t % 2:t % 2 + 1, :], ALU.add).then_inc(x2_ready, 1)

            def divide_by_sum(it, u):
                wait(pool, rinv_ready, it, u + 1)
                nc.gpsimd.tensor_scalar(prob[:, u % 3, :], prob[:, u % 3, :], rinv[:, u:u + 1], 1.0,
                                        ALU.mult, ALU.mult).then_inc(pnorm_ready, 1)

            for it in range(B):
                inv_std(it, 0)
                inv_std(it, 1)
                for u in range(T):
                    divide_by_sum(it, u)
                for t in range(T):
                    attn_const(it, t)
                for t in range(T - 3):
                    attn_residual(it, t)
                inv_std(it, 2)
                attn_residual(it, T - 3)
                attn_residual(it, T - 2)
                for n in range(HC):
                    gelu_high(it, n)
                    if n == 1:
                        attn_residual(it, T - 1)
                    if n == 3:
                        inv_std(it, 3)
                    if n >= 4:
                        x2_const(it, n - 4)
                for t in range(TH):
                    result(it, t)
                for n in range(HC, 2 * HC):
                    gelu_high(it, n)
                    if n >= HC + 4:
                        x2_const(it, n - HC)
                for t in range(TH, T):
                    result(it, t)

        @block.scalar
        def _(act):
            act.dma_start(wattn_raw[:, :, :], w_attn.rearrange("(c p) n -> p c n", p=P)).then_inc(wattn_in, 16)
            act.dma_start(wvt_raw[:, :, :], wv_t.rearrange("(c p) n -> p c n", p=P)).then_inc(wvt_in, 16)
            act.dma_start(wp_raw[:, :, :], wp.rearrange("(c p) n -> p c n", p=P)).then_inc(wp_in, 16)
            act.dma_start(rows_raw[:, :], rows).then_inc(rows_in, 16)
            act.wait_ge(cols_in, 16)
            nc.scalar.activation(small[:, 0:4], cols_sb[:, C_CT:C_CT + 4], ACT.Exp, scale=-1.0).then_inc(pre_act, 1)
            act.wait_ge(pre_dve, 1)
            nc.scalar.activation(small[:, 4:5], small[:, 5:6], ACT.Exp, scale=-1.0).then_inc(pre_act, 1)
            act.wait_ge(wattn_in, 16)
            nc.scalar.activation(wqk_hi[:, :, :], wattn_raw[:, :, 0:2 * E], ACT.Copy).then_inc(wprep_hi, 1)
            nc.scalar.activation(wv_hi[:, :, 0:DK], wattn_raw[:, :, 2 * E:2 * E + DK], ACT.Copy).then_inc(wprep_hi, 1)
            act.wait_ge(wvp_psum, 1)
            nc.scalar.activation(wv_hi[:, :, DK:NV], a_ps[0][:, :].rearrange("p (c n) -> p c n", c=EC), ACT.Copy)\
                .then_inc(wprep_hi, 1)

            def affine(it, r):
                wait(act, ht_psum, it, r + 1)
                if r >= 2:
                    wait(act, hlo_ready, it, r - 1)
                if r == 0:
                    wait(act, modb_ready, it, 1)
                o = 0 if r < 4 else 4
                c = r % 2
                nc.scalar.activation(h32[:, r % 2, :], t_bank("h", r)[:, :], ACT.Identity,
                                     scale=modb[:, o + 2 + c:o + 3 + c], bias=modb[:, o + c:o + 1 + c])\
                    .then_inc(h32_ready, 1)

            def qk_bias(it, j):
                m, h = QK_JOBS[j]
                wait(act, qk_psum, it, j + 1)
                if j >= 3:
                    wait(act, qklo_ready, it, j - 2)
                src = s_bank(j) if j < 4 else a_bank("qk", j)[:, :]
                if m < 2:
                    a = nc.scalar.activation(f32s[:, j % 3, :], src, ACT.Identity, scale=QSCALE, bias=small[:, 8 + m:9 + m])
                else:
                    a = nc.scalar.activation(f32s[:, j % 3, :], src, ACT.Identity,
                                             bias=cols_sb[:, C_BK + m - 2:C_BK + m - 1])
                a.then_inc(qk32_ready, 1)

            def v_high(it, t):
                wait(act, v_psum, it, t + 1)
                nc.scalar.activation(v_hi[:, t, :], a_bank("v", t)[:, 0:NV], ACT.Copy).then_inc(vhi_ready, 1)

            def prob_high(it, u):
                for b in range(2):
                    wait(act, t_psum, it, 2 * u + b + 1)
                    if u == 2:
                        act.wait_ge(wffn_lo, 2)
                    nc.scalar.activation(pt_hi[:, (u // 2) % 2, 4 * b:4 * b + 4, (u % 2) * P:(u % 2 + 1) * P],
                                         t_bank("p", 2 * u + b)[:, :].rearrange("p (t n) -> p t n", n=P),
                                         ACT.Copy).then_inc(pthi_ready, 1)

            def softmax_exp(it, u):
                wait(act, nmax_ready, it, u + 1)
                if u >= 3:
                    wait(act, t_psum, it, 2 * (u - 2))
                nc.scalar.activation(prob[:, u % 3, :], s_ps[u % 2][:, :], ACT.Exp, bias=nmax[:, u:u + 1],
                                     accum_out=rsum[:, u:u + 1]).then_inc(exp_ready, 1)

            def gelu(it, n):
                wait(act, f1_psum, it, n + 1)
                if n >= 3:
                    wait(act, glo_ready, it, n - 2)
                nc.scalar.activation(f32s[:, n % 3, :], s_bank(n % 4), ACT.Gelu,
                                     bias=cols_sb[:, C_B1 + n % HC:C_B1 + n % HC + 1]).then_inc(gelu_ready, 1)

            for it in range(B):
                for r in range(4):
                    affine(it, r)
                for j in range(4):
                    qk_bias(it, j)
                for s in range(UNITS + 2):
                    if s >= 2:
                        prob_high(it, s - 2)
                    if s < UNITS:
                        softmax_exp(it, s)
                    if s < 2:
                        for t in range(4 * s, 4 * s + 4):
                            v_high(it, t)
                    elif s < 6:
                        qk_bias(it, s + 2)
                    if s >= 4 and s % 2 == 0 and s <= 10:
                        p = (s - 4) // 2
                        wait(act, ctx_psum, it, p + 1)
                        if p >= 2:
                            wait(act, qplo_ready, it, p - 1)
                        nc.scalar.activation(th[:, p % 2, :], a_bank("ctx", p)[:, 0:2 * P], ACT.Tanh,
                                             scale=cols_sb[:, C_GATE:C_GATE + 1], bias=small[:, 10:11])\
                            .then_inc(tanh_ready, 1)
                    if s == 16:
                        affine(it, 4)
                        affine(it, 5)
                for n in range(HC):
                    gelu(it, n)
                affine(it, 6)
                affine(it, 7)
                for n in range(HC, 2 * HC):
                    gelu(it, n)

        @block.vector
        def _(dve):
            V = nc.vector
            dve.wait_ge(cols_in, 16)
            V.tensor_scalar(small[:, 5:6], cols_sb[:, C_W1:C_W1 + 1], DEPTH, cols_sb[:, C_W0:C_W0 + 1],
                            ALU.mult, ALU.add).then_inc(pre_dve, 1)
            V.tensor_scalar(small[:, 8:10], cols_sb[:, C_BQ:C_BQ + 2], QSCALE, None, ALU.mult)
            V.tensor_tensor(small[:, 10:11], cols_sb[:, C_BVC:C_BVC + 1], cols_sb[:, C_GATE:C_GATE + 1], ALU.mult)
            V.tensor_copy(bvb[:, :, :], cols_sb[:, C_BV:C_BV + 2].rearrange("p (c a) -> p c a", a=1)
                          .to_broadcast([P, EC, P]))
            dve.wait_ge(pre_act, 2)
            V.tensor_scalar(small[:, 0:5], small[:, 0:5], 1.0, None, ALU.add).then_inc(pre_dve, 1)
            dve.wait_ge(pre_dve, 2)
            V.reciprocal(small[:, 0:5], small[:, 0:5]).then_inc(pre_dve, 1)
            dve.wait_ge(pre_dve, 3)
            V.tensor_tensor(sct[:, :, :], cols_sb[:, C_CT:C_CT + 4].rearrange("p (c b) -> p c b", b=B),
                            small[:, 0:4].rearrange("p (c b) -> p c b", b=B), ALU.mult).then_inc(pre_dve, 1)
            V.tensor_scalar(small[:, 11:12], small[:, 4:5], QSCALE, None, ALU.mult)
            dve.wait_ge(pre_dve, 4)
            V.tensor_copy(scb[:, :, :, :].rearrange("p c b n -> p (c b) n"),
                          sct[:, :, :].rearrange("p c b -> p (c b)").rearrange("p (m a) -> p m a", a=1)
                          .to_broadcast([P, EC * B, P])).then_inc(silu_ready, 1)
            dve.wait_ge(modt_psum, 1)
            mt = t_ps[0][:, 0:16].rearrange("p (b v) -> p b v", b=B)
            V.tensor_copy(modc[:, :, :], mt).then_inc(pre_dve, 1)
            dve.wait_ge(pre_dve, 5)
            mc = modc[:, :, :].rearrange("p b (v k) -> p (b v) k", k=4)[:, :, 2:4]
            V.tensor_scalar(mc, mc, 1.0, None, ALU.add).then_inc(pre_dve, 1)
            gtmp = f32s[:, 0:2, :].rearrange("p a n -> p (a n)")
            dve.wait_ge(gate_psum, 1)
            V.tensor_scalar(gtmp, s_ps[0][:, :], 2.0, None, ALU.mult).then_inc(pre_dve, 1)
            dve.wait_ge(pre_dve, 7)
            gv = gates[:, :, :, :].rearrange("p b v n -> p (b v n)")
            V.scalar_tensor_tensor(gv, gtmp, -1.0, gtmp, ALU.mult, ALU.max).then_inc(pre_dve, 1)
            dve.wait_ge(pre_dve, 8)
            V.tensor_scalar(gtmp, s_ps[0][:, :], 0.0, -0.5, ALU.is_ge, ALU.add).then_inc(pre_dve, 1)
            dve.wait_ge(pre_dve, 9)
            V.scalar_tensor_tensor(gv, gv, 0.5, gtmp, ALU.max, ALU.mult).then_inc(pre_dve, 1)
            dve.wait_ge(wprep_hi, 1)
            V.tensor_tensor(wqk_lo[:, :, :], wattn_raw[:, :, 0:2 * E], f(wqk_hi[:, :, :]), ALU.subtract).then_inc(wprep_lo, 1)
            dve.wait_ge(wprep_hi, 2)
            V.tensor_tensor(wv_lo[:, :, 0:DK], wattn_raw[:, :, 2 * E:2 * E + DK], f(wv_hi[:, :, 0:DK]), ALU.subtract)\
                .then_inc(wprep_lo, 1)
            dve.wait_ge(wprep_hi, 3)
            V.tensor_tensor(wv_lo[:, :, DK:NV], a_ps[0][:, :].rearrange("p (c n) -> p c n", c=EC),
                            f(wv_hi[:, :, DK:NV]), ALU.subtract).then_inc(wprep_lo, 1)
            dve.wait_ge(row_psum, 1)
            dve.wait_ge(pre_dve, 10)
            for b in range(B):
                last = V.tensor_tensor(consts[:, b, :, :], a_ps[1][:, :].rearrange("p (v n) -> p v n", v=2),
                                       gates[:, b, :, :], ALU.mult)
            last.then_inc(pre_dve, 1)

            def norm(it, n, stats=True):
                h = n % 2
                if stats:
                    for t in range(h * TH, (h + 1) * TH):
                        if n >= 2:
                            wait(dve, x2_ready, it, t + 1)
                        last = V.bn_stats(bst[:, t, :], x_all[:, bass.ds(it * T + t, 1), :])
                    last.then_inc(bst_ready, 1)
                    wait(dve, bst_ready, it, n + 1)
                    for t in range(h * TH, (h + 1) * TH):
                        last = V.bn_aggr(mv[:, t, :], bst[:, t, :])
                    last.then_inc(mv_ready, 1)
                    wait(dve, mv_ready, it, n + 1)
                    V.tensor_scalar(ve[:, h * TH:(h + 1) * TH], mv[:, h * TH:(h + 1) * TH, 1], EPS, None, ALU.add)\
                        .then_inc(ve_ready, 1)
                else:
                    wait(dve, rstd_ready, it, n + 1)
                    if n:
                        wait(dve, ht_psum, it, 2 * n)
                    for t in range(TH):
                        j = h * TH + t
                        last = V.tensor_scalar(xn[:, t:t + 1, :], x_all[:, bass.ds(it * T + j, 1), :], mv[:, j, 0:1],
                                               rstd[:, j:j + 1], ALU.subtract, ALU.mult)
                    last.then_inc(xn_ready, 1)

            def h_split(it, r):
                h, c = (r // 2) % 2, r % 2
                wait(dve, h32_ready, it, r + 1)
                dst = (slice(None), c, slice(h * HALF, (h + 1) * HALF))
                V.tensor_copy(ht_hi[dst], h32[:, r % 2, :]).then_inc(hhi_ready, 1)
                wait(dve, hhi_ready, it, r + 1)
                V.tensor_tensor(ht_lo[dst], h32[:, r % 2, :], f(ht_hi[dst]), ALU.subtract).then_inc(hlo_ready, 1)

            def qk_split(it, j):
                m, h = QK_JOBS[j]
                hi, lo = (q_hi, q_lo) if m < 2 else (k_hi, k_lo)
                dst = (slice(None), m % 2, slice(h * HALF, (h + 1) * HALF))
                wait(dve, qk32_ready, it, j + 1)
                V.tensor_copy(hi[dst], f32s[:, j % 3, :]).then_inc(qkhi_ready, 1)
                wait(dve, qkhi_ready, it, j + 1)
                V.tensor_tensor(lo[dst], f32s[:, j % 3, :], f(hi[dst]), ALU.subtract).then_inc(qklo_ready, 1)

            def q_update(it, p):
                dst = (slice(None), 0, slice(2 * P * p, 2 * P * (p + 1)))
                t = th[:, p % 2, :]
                wait(dve, tanh_ready, it, p + 1)
                V.scalar_tensor_tensor(t, t, small[:, 11:12], f(q_lo[dst]), ALU.mult, ALU.add).then_inc(qcam_ready, 1)
                wait(dve, qcam_ready, it, 2 * p + 1)
                V.tensor_tensor(t, t, f(q_hi[dst]), ALU.add).then_inc(qcam_ready, 1)
                wait(dve, qcam_ready, it, 2 * p + 2)
                V.tensor_copy(q_hi[dst], t).then_inc(qphi_ready, 1)
                wait(dve, qphi_ready, it, p + 1)
                V.tensor_tensor(q_lo[dst], t, f(q_hi[dst]), ALU.subtract).then_inc(qplo_ready, 1)

            def prob_low(it, u):
                for b in range(2):
                    wait(dve, pthi_ready, it, 2 * u + b + 1)
                    dst = (slice(None), (u // 2) % 2, slice(4 * b, 4 * b + 4), slice((u % 2) * P, (u % 2 + 1) * P))
                    V.tensor_tensor(pt_lo[dst], t_bank("p", 2 * u + b)[:, :].rearrange("p (t n) -> p t n", n=P),
                                    f(pt_hi[dst]), ALU.subtract).then_inc(ptlo_ready, 1)

            def gated(it, i, kind):
                if kind == "pv":
                    wait(dve, pv_psum, it, i + 1)
                    if i >= 2:
                        wait(dve, x2_ready, it, i - 1)
                    V.scalar_tensor_tensor(o1[:, i % 2:i % 2 + 1, :],
                                           a_bank("pv", i)[:, 0:E].rearrange("p (a n) -> p a n", a=1),
                                           rinv[:, T + i:T + i + 1], gates[:, bass.ds(it, 1), 0, :],
                                           ALU.mult, ALU.mult).then_inc(o1_ready, 1)
                else:
                    wait(dve, f2_psum, it, i + 1)
                    if i >= 2:
                        wait(dve, y_ready, it, i - 1)
                    else:
                        wait(dve, x2_ready, it, T - 1 + i)
                    V.tensor_tensor(o1[:, i % 2:i % 2 + 1, :],
                                    a_bank("f2", i)[:, 0:E].rearrange("p (a n) -> p a n", a=1),
                                    gates[:, bass.ds(it, 1), 1, :], ALU.mult).then_inc(t2_ready, 1)

            def gelu_low(it, n):
                wait(dve, ghi_ready, it, n + 1)
                V.tensor_tensor(gt_lo[:, n % HC, :], f32s[:, n % 3, :], f(gt_hi[:, n % HC, :]), ALU.subtract)\
                    .then_inc(glo_ready, 1)

            dve.wait_ge(const_ready, 2)
            for h in range(2 * B):
                dve.wait_ge(x_in[h], 16)
            dve.wait_ge(pre_dve, 11)
            for it in range(B):
                V.tensor_copy(modb[:, :], modc[:, bass.ds(it, 1), :].rearrange("p a n -> p (a n)")).then_inc(modb_ready, 1)
                norm(it, 0)
                norm(it, 0, stats=False)
                norm(it, 1)
                h_split(it, 0)
                h_split(it, 1)
                norm(it, 1, stats=False)
                h_split(it, 2)
                h_split(it, 3)
                for j in range(4):
                    qk_split(it, j)
                for s in range(UNITS + 2):
                    if s < UNITS:
                        wait(dve, s_psum, it, s + 1)
                        V.tensor_reduce(nmax[:, s:s + 1], s_ps[s % 2][:, :], AX.X, ALU.max, negate=True)\
                            .then_inc(nmax_ready, 1)
                    if s < 2:
                        for t in range(4 * s, 4 * s + 4):
                            wait(dve, vhi_ready, it, t + 1)
                            V.tensor_tensor(v_lo[:, t, :], a_bank("v", t)[:, 0:NV], f(v_hi[:, t, :]), ALU.subtract)\
                                .then_inc(vlo_ready, 1)
                    if s == UNITS:
                        norm(it, 2, stats=False)
                    if s == UNITS + 1:
                        h_split(it, 4)
                        h_split(it, 5)
                    if s >= T + 3:
                        gated(it, s - T - 3, "pv")
                    if 2 <= s < UNITS + 2:
                        prob_low(it, s - 2)
                    if s < UNITS:
                        wait(dve, exp_ready, it, s + 1)
                        V.reciprocal(rinv[:, s:s + 1], rsum[:, s:s + 1]).then_inc(rinv_ready, 1)
                    if 2 <= s < 6:
                        qk_split(it, s + 2)
                    if s >= 4 and s % 2 == 0 and s <= 10:
                        q_update(it, (s - 4) // 2)
                    if s == UNITS - 1:
                        norm(it, 2)
                for n in range(HC):
                    gelu_low(it, n)
                    if n == 1:
                        gated(it, T - 1, "pv")
                    if n == 2:
                        norm(it, 3)
                    if n == 4:
                        norm(it, 3, stats=False)
                h_split(it, 6)
                h_split(it, 7)
                for t in range(TH):
                    gated(it, t, "f2")
                for n in range(HC, 2 * HC):
                    gelu_low(it, n)
                for t in range(TH, T):
                    gated(it, t, "f2")

        @block.tensor
        def _(pe):
            M = nc.tensor.matmul
            pe.wait_ge(wvt_in, 16)
            pe.wait_ge(wp_in, 16)
            for m in range(EC):
                for k in range(EC):
                    last = M(a_ps[0][:, m * E:(m + 1) * E], wvt_raw[:, k, m * P:(m + 1) * P], wp_raw[:, k, :],
                             start=k == 0, stop=k == EC - 1)
            last.then_inc(wvp_psum, 1)
            pe.wait_ge(rows_in, 16)
            pe.wait_ge(const_ready, 2)
            pe.wait_ge(silu_ready, 1)
            for k in range(EC):
                M(a_ps[1][:, 0:E], bvb[:, k, :], wp_raw[:, k, :], start=k == 0, stop=False)
            M(a_ps[1][:, 0:E], ones_row[0:1, :], rows_raw[0:1, 0:E], start=False, stop=True)
            M(a_ps[1][:, E:2 * E], ones_row[0:1, :], rows_raw[0:1, E:2 * E], start=True, stop=True).then_inc(row_psum, 1)
            pe.wait_ge(wmod_in, 16)
            mt = t_ps[0][:, 0:16].rearrange("p (b v) -> p b v", b=B)
            for v in range(8):
                col = (0, 1, 3, 4)[v // 2] * E + (v % 2) * P
                for k in range(EC):
                    last = M(mt[:, :, v], wmod_raw[:, k, col:col + P], sct[:, k, :], start=k == 0, stop=k == EC - 1)
            last.then_inc(modt_psum, 1)
            for b in range(B):
                for v, col in enumerate((2 * E, 5 * E)):
                    o = (b * 2 + v) * E
                    for k in range(EC):
                        last = M(s_ps[0][:, o:o + E], scb[:, k, b, :], wmod_raw[:, k, col:col + E],
                                 start=k == 0, stop=k == EC - 1)
            last.then_inc(gate_psum, 1)
            pe.wait_ge(ident_ready, 1)

            def a_free(it, kind, k):
                n = A_JOBS.index((kind, k))
                if n >= 2:
                    what, j = A_JOBS[n - 2]
                    wait(pe, READ_OUT[what], it, j + 1)

            def t_free(it, kind, k):
                n = T_JOBS.index((kind, k))
                if n >= 2:
                    what, j = T_JOBS[n - 2]
                    wait(pe, T_READ_OUT[what], it, j + 1)

            def h_transpose(it, r):
                wait(pe, xn_ready, it, r // 2 + 1)
                t_free(it, "h", r)
                c = r % 2
                for t in range(TH):
                    last = nc.tensor.transpose(t_bank("h", r)[:, t * P:(t + 1) * P], xn[:, t, c * P:(c + 1) * P],
                                               ident[:, :])
                last.then_inc(ht_psum, 1)

            def qk_project(it, j):
                m, h = QK_JOBS[j]
                if j < 4:
                    wait(pe, hlo_ready, it, 2 * h + 2)
                    o = s_bank(j)
                else:
                    a_free(it, "qk", j)
                    o = a_bank("qk", j)[:, :]
                n = slice(h * HALF, (h + 1) * HALF)
                for k in range(EC):
                    last = mm3(o, wqk_hi[:, k, m * P:(m + 1) * P], wqk_lo[:, k, m * P:(m + 1) * P],
                               ht_hi[:, k, n], ht_lo[:, k, n], k == 0, k == EC - 1)
                last.then_inc(qk_psum, 1)

            def v_project(it, t):
                a_free(it, "v", t)
                n = slice(t * P, (t + 1) * P)
                for k in range(EC):
                    last = mm3(a_bank("v", t)[:, 0:NV], ht_hi[:, k, n], ht_lo[:, k, n], wv_hi[:, k, :], wv_lo[:, k, :],
                               k == 0, k == EC - 1)
                last.then_inc(v_psum, 1)

            def scores(it, u):
                n = slice((u % T) * P, (u % T + 1) * P)
                if u == 0:
                    wait(pe, qklo_ready, it, 4)
                if u >= 2:
                    wait(pe, exp_ready, it, u - 1)
                if u == T:
                    wait(pe, qklo_ready, it, 8)
                if u >= T and u % 2 == 0:
                    wait(pe, qplo_ready, it, (u - T) // 2 + 1)
                chunks = 1 if u < T else EC
                for b in range(2):
                    cols_b = slice(b * HALF, (b + 1) * HALF)
                    for k in range(chunks):
                        last = mm3(s_ps[u % 2][:, cols_b], q_hi[:, k, n], q_lo[:, k, n], k_hi[:, k, cols_b],
                                   k_lo[:, k, cols_b], k == 0, k == chunks - 1)
                last.then_inc(s_psum, 1)

            def transpose_probs(it, u):
                wait(pe, pnorm_ready if u < T else exp_ready, it, u + 1)
                for b in range(2):
                    t_free(it, "p", 2 * u + b)
                    for t in range(4):
                        c = (4 * b + t) * P
                        last = nc.tensor.transpose(t_bank("p", 2 * u + b)[:, t * P:(t + 1) * P],
                                                   prob[:, u % 3, c:c + P], ident[:, :])
                    last.then_inc(t_psum, 1)

            def cam_context(it, p):
                if p == 0:
                    wait(pe, vlo_ready, it, T)
                wait(pe, ptlo_ready, it, 4 * p + 4)
                a_free(it, "ctx", p)
                for t in range(T):
                    last = mm3(a_bank("ctx", p)[:, 0:2 * P], v_hi[:, t, 0:DK], v_lo[:, t, 0:DK],
                               pt_hi[:, p % 2, t, :], pt_lo[:, p % 2, t, :], t == 0, t == T - 1)
                last.then_inc(ctx_psum, 1)

            def attend(it, i):
                u = T + i
                wait(pe, ptlo_ready, it, 2 * u + 2)
                a_free(it, "pv", i)
                n = slice((u % 2) * P, (u % 2 + 1) * P)
                for t in range(T):
                    last = mm3(a_bank("pv", i)[:, 0:E], pt_hi[:, (u // 2) % 2, t, n], pt_lo[:, (u // 2) % 2, t, n],
                               v_hi[:, t, DK:NV], v_lo[:, t, DK:NV], t == 0, t == T - 1)
                last.then_inc(pv_psum, 1)

            def ffn_up(it, n):
                h, c = n // HC, n % HC
                if c == 0:
                    wait(pe, hlo_ready, it, 6 + 2 * h)
                if n < 4:
                    wait(pe, exp_ready, it, UNITS - 1 + n // 2)
                else:
                    wait(pe, gelu_ready, it, n - 3)
                cols_h = slice(h * HALF, (h + 1) * HALF)
                for k in range(EC):
                    last = mm3(s_bank(n % 4), w1_hi[:, k, c * P:(c + 1) * P], w1_lo[:, k, c * P:(c + 1) * P],
                               ht_hi[:, k, cols_h], ht_lo[:, k, cols_h], k == 0, k == EC - 1)
                last.then_inc(f1_psum, 1)

            def ffn_down(it, i):
                a_free(it, "f2", i)
                n = slice((i % TH) * P, (i % TH + 1) * P)
                for c in range(HC):
                    if i % TH == 0:
                        wait(pe, glo_ready, it, (i // TH) * HC + c + 1)
                    last = mm3(a_bank("f2", i)[:, 0:E], gt_hi[:, c, n], gt_lo[:, c, n], w2_hi[:, c, :], w2_lo[:, c, :],
                               c == 0, c == HC - 1)
                last.then_inc(f2_psum, 1)

            pe.wait_ge(wprep_lo, 3)
            for it in range(B):
                for r in range(4):
                    h_transpose(it, r)
                for j in range(4):
                    qk_project(it, j)
                for s in range(UNITS + 2):
                    if s < UNITS:
                        scores(it, s)
                    if s < 2:
                        for t in range(4 * s, 4 * s + 4):
                            v_project(it, t)
                    if s == UNITS + 1:
                        h_transpose(it, 4)
                        h_transpose(it, 5)
                    if s >= 4 and s % 2 == 0 and s <= 10:
                        cam_context(it, (s - 4) // 2)
                    if 2 <= s < 6:
                        qk_project(it, s + 2)
                    if s >= T + 3:
                        attend(it, s - T - 3)
                    if s >= 2:
                        transpose_probs(it, s - 2)
                pe.wait_ge(wffn_lo, 2)
                for n in range(HC):
                    ffn_up(it, n)
                    if n == 1:
                        attend(it, T - 1)
                h_transpose(it, 6)
                h_transpose(it, 7)
                for i in range(TH):
                    ffn_down(it, i)
                for n in range(HC, 2 * HC):
                    ffn_up(it, n)
                for i in range(TH, T):
                    ffn_down(it, i)


def kernel(L0_attn_hidden_states, L0_attn_c_attn_w, L0_attn_c_attn_b, L0_attn_c_proj_w, L0_attn_c_proj_b,
           L0_attn_cam_gate, L0_attn_cam_w0, L0_attn_cam_w1, L0_ffn_proj1, L0_ffn_proj1_bias, L0_ffn_proj2,
           L0_ffn_proj2_bias, L0_ffn_gate_w, L0_c, L0_wmod):
    import numpy as np
    import concourse.bacc as bacc
    from concourse.bass_utils import run_bass_kernel_spmd

    def columns(v):
        return np.asarray(v).reshape(-1, P).T

    w_attn, b_attn = np.asarray(L0_attn_c_attn_w), np.asarray(L0_attn_c_attn_b)
    ct = np.asarray(L0_c).T.reshape(EC, P, B).transpose(1, 0, 2).reshape(P, EC * B)
    cols = np.concatenate([
        ct, columns(b_attn[0:E]), columns(b_attn[E:2 * E]), columns(b_attn[2 * E:2 * E + DK]), columns(b_attn[2 * E:]),
        columns(L0_attn_cam_gate), columns(L0_ffn_proj1_bias),
        np.broadcast_to(np.asarray(L0_attn_cam_w0), (P, 1)), np.broadcast_to(np.asarray(L0_attn_cam_w1), (P, 1))], axis=1)
    rows = np.concatenate([np.asarray(L0_attn_c_proj_b), np.asarray(L0_ffn_proj2_bias)]).reshape(1, 2 * E)
    arrays = {
        "x": np.asarray(L0_attn_hidden_states),
        "cols": cols,
        "wmod": np.asarray(L0_wmod),
        "w_attn": w_attn,
        "wv_t": w_attn[:, 2 * E:].T,
        "wp": np.asarray(L0_attn_c_proj_w),
        "rows": rows,
        "w1_t": np.asarray(L0_ffn_proj1).T,
        "w2_t": np.asarray(L0_ffn_proj2).T,
    }
    arrays = {n: np.ascontiguousarray(a) for n, a in arrays.items()}
    nc = bacc.Bacc("TRN2", target_bir_lowering=False, num_devices=1)
    args = [nc.dram_tensor(n, a.shape, mybir.dt.from_np(a.dtype), kind="ExternalInput").ap() for n, a in arrays.items()]
    out = nc.dram_tensor("out", (B, S, E), F32, kind="ExternalOutput").ap()
    adaln_block_kernel(nc, *args, out)
    r = run_bass_kernel_spmd(nc, [arrays], core_ids=[0])
    return r.results[0]["out"]
```

```python
import concourse.bass as bass
from concourse import mybir
from contextlib import ExitStack

F32 = mybir.dt.float32
F32R = mybir.dt.float32r
ACT = mybir.ActivationFunctionType
ALU = mybir.AluOpType
AX = mybir.AxisListType

P = 128
B, S, E, H = 2, 1024, 256, 1024
DK = 128
EC, HC = E // P, H // P
T = S // P
HALF = 512
TH = HALF // P
QSCALE = 0.25
EPS = 1e-5
DEPTH = 0.5
NV = DK + E
UNITS = 2 * T

C_CT, C_BQ, C_BK, C_BVC, C_BV, C_GATE, C_B1, C_W0, C_W1 = 0, 4, 6, 8, 9, 11, 12, 20, 21
NCOLS = 22


def adaln_block_kernel(nc, x, cols, wmod, w_attn, wv_t, wp, rows, w1_t, w2_t, out):
    x_v = x.rearrange("b (t p) e -> p (b t) e", p=P)
    out_v = out.rearrange("b (t p) e -> p (b t) e", p=P)

    ctx = ExitStack()
    raw, raw_ffn = ExitStack(), ExitStack()
    with ctx:
        def sb(name, shape, dt=F32, scope=ctx):
            return scope.enter_context(nc.sbuf_tensor(name, shape, dt))

        def sem(name):
            return ctx.enter_context(nc.semaphore(name))

        x_all = sb("x_all", [P, B * T, E])
        ident = sb("ident", [P, P])
        cols_sb = sb("cols_sb", [P, NCOLS])
        exps = sb("exps", [P, EC * B + 1])
        lw_arg = sb("lw_arg", [P, 1])
        lw_scaled = sb("lw_scaled", [P, 1])
        bq_scaled = sb("bq_scaled", [P, EC])
        gate_bias = sb("gate_bias", [P, 1])
        minus_half = sb("minus_half", [P, TH])
        modc = sb("modc", [P, B, 8])
        gates = sb("gates", [P, B, 2, E])
        consts = sb("consts", [P, B, 2, E])
        wqk_hi, wqk_lo = (sb(f"wqk_{n}", [P, EC, 2 * E], F32R) for n in ("hi", "lo"))
        wv_hi, wv_lo = (sb(f"wv_{n}", [P, EC, NV], F32R) for n in ("hi", "lo"))
        w1_hi, w1_lo = (sb(f"w1_{n}", [P, EC, H], F32R) for n in ("hi", "lo"))
        w2_hi, w2_lo = (sb(f"w2_{n}", [P, HC, E], F32R) for n in ("hi", "lo"))
        bst = sb("bst", [P, T, 6])
        mv = sb("mv", [P, T, 2])
        ve = sb("ve", [P, T])
        rstd = sb("rstd", [P, T])
        xn = sb("xn", [P, TH, E])
        h32 = sb("h32", [P, 2, HALF])
        f32s = sb("f32s", [P, 3, HALF])
        q_hi, q_lo = (sb(f"q_{n}", [P, EC, S], F32R) for n in ("hi", "lo"))
        k_hi, k_lo = (sb(f"k_{n}", [P, EC, S], F32R) for n in ("hi", "lo"))
        v_hi, v_lo = (sb(f"v_{n}", [P, T, NV], F32R) for n in ("hi", "lo"))
        nmax = sb("nmax", [P, UNITS])
        rsum = sb("rsum", [P, UNITS])
        rinv = sb("rinv", [P, UNITS])
        th = sb("th", [P, 2, 2 * P])
        o1 = sb("o1", [P, 2, E])
        prob = sb("prob", [P, 3, S])

        with raw_ffn:
            w1_raw = sb("w1_raw", [P, EC, H], scope=raw_ffn)
            w2_raw = sb("w2_raw", [P, HC, E], scope=raw_ffn)
        ht_hi, ht_lo = (sb(f"ht_{n}", [P, EC, S], F32R) for n in ("hi", "lo"))

        with raw:
            wattn_raw = sb("wattn_raw", [P, EC, 3 * E], scope=raw)
            wvt_raw = sb("wvt_raw", [P, EC, E], scope=raw)
            wp_raw = sb("wp_raw", [P, EC, E], scope=raw)
            wmod_raw = sb("wmod_raw", [P, EC, 6 * E], scope=raw)
            rows_raw = sb("rows_raw", [1, 2 * E], scope=raw)
            sct = sb("sct", [P, EC, B], scope=raw)
            scb = sb("scb", [P, EC, B, P], scope=raw)
            bvb = sb("bvb", [P, EC, P], scope=raw)
            ones_row = sb("ones_row", [1, P], scope=raw)
        pt_hi, pt_lo = (sb(f"pt_{n}", [P, 2, T, 2 * P], F32R) for n in ("hi", "lo"))
        gt_hi, gt_lo = (a[:, :, :, :].rearrange("p a t n -> p (a t n)")
                        .rearrange("p (h n) -> p h n", n=HALF) for a in (pt_hi, pt_lo))

        s_ps = [ctx.enter_context(nc.psum_tensor(f"s_ps{i}", [P, 2 * HALF], F32)) for i in range(2)]
        t_ps = [ctx.enter_context(nc.psum_tensor(f"t_ps{i}", [P, HALF], F32)) for i in range(2)]
        a_ps = [ctx.enter_context(nc.psum_tensor(f"a_ps{i}", [P, HALF], F32)) for i in range(2)]

        def s_bank(k):
            return s_ps[k // 2][:, (k % 2) * HALF:(k % 2 + 1) * HALF]

        def f(ap):
            return ap.bitcast(F32)

        cols_in, wmod1_in, wmod2_in, wqk_in, wv_in, wvt_in, wp_in, rows_in, w1_in, w2_in = (
            sem(n) for n in ("cols_in", "wmod1_in", "wmod2_in", "wqk_in", "wv_in", "wvt_in", "wp_in", "rows_in",
                             "w1_in", "w2_in"))
        x_in = [sem(f"x_in{i}") for i in range(2 * B)]
        const_ready, ident_ready, bias_ready, lw_ready, exps_ready, plus1_ready, recip_ready, sct_ready, silu_ready, \
            mod1_psum, mod2_psum, mod_copied, mod_ready, gate_psum, gate_copied, gate_abs, gate_sign, gates_ready, \
            wvp_psum, row_psum, rows_copied, const_other, consts_ready, wqk_hi_ready, wqk_lo_ready, \
            wv_hi_ready, wv_lo_ready, wffn_hi, wffn_lo = (
                sem(n) for n in ("const_ready", "ident_ready", "bias_ready", "lw_ready", "exps_ready", "plus1_ready",
                                 "recip_ready", "sct_ready", "silu_ready", "mod1_psum", "mod2_psum", "mod_copied",
                                 "mod_ready", "gate_psum", "gate_copied", "gate_abs", "gate_sign", "gates_ready",
                                 "wvp_psum", "row_psum", "rows_copied", "const_other", "consts_ready",
                                 "wqk_hi_ready", "wqk_lo_ready", "wv_hi_ready", "wv_lo_ready", "wffn_hi", "wffn_lo"))

        per = {}

        def lsem(name, n):
            s = sem(name)
            per[s] = n
            return s

        bst_ready = lsem("bst_ready", 4)
        mv_ready = lsem("mv_ready", 4)
        ve_ready = lsem("ve_ready", 4)
        rstd_ready = lsem("rstd_ready", 4)
        xn_ready = lsem("xn_ready", 4)
        ht_psum = lsem("ht_psum", 8)
        h32_ready = lsem("h32_ready", 8)
        hhi_ready = lsem("hhi_ready", 8)
        hlo_ready = lsem("hlo_ready", 8)
        qk_psum = lsem("qk_psum", 8)
        qk32_ready = lsem("qk32_ready", 8)
        qkhi_ready = lsem("qkhi_ready", 8)
        qklo_ready = lsem("qklo_ready", 8)
        v_psum = lsem("v_psum", T)
        vhi_ready = lsem("vhi_ready", T)
        vlo_ready = lsem("vlo_ready", T)
        s_psum = lsem("s_psum", UNITS)
        nmax_ready = lsem("nmax_ready", UNITS)
        exp_ready = lsem("exp_ready", UNITS)
        rinv_ready = lsem("rinv_ready", UNITS)
        pnorm_ready = lsem("pnorm_ready", T)
        t_psum = lsem("t_psum", 2 * UNITS)
        pthi_ready = lsem("pthi_ready", 2 * UNITS)
        ptlo_ready = lsem("ptlo_ready", 2 * UNITS)
        ctx_psum = lsem("ctx_psum", T // 2)
        tanh_ready = lsem("tanh_ready", T // 2)
        qcam_ready = lsem("qcam_ready", T)
        qphi_ready = lsem("qphi_ready", T // 2)
        qplo_ready = lsem("qplo_ready", T // 2)
        pv_psum = lsem("pv_psum", T)
        o1_ready = lsem("o1_ready", T)
        xc_ready = lsem("xc_ready", T)
        x2_ready = lsem("x2_ready", T)
        x2c_ready = lsem("x2c_ready", T)
        f1_psum = lsem("f1_psum", 2 * HC)
        gelu_ready = lsem("gelu_ready", 2 * HC)
        ghi_ready = lsem("ghi_ready", 2 * HC)
        glo_ready = lsem("glo_ready", 2 * HC)
        f2_psum = lsem("f2_psum", T)
        t2_ready = lsem("t2_ready", T)
        y_ready = lsem("y_ready", T)
        y_out = sem("y_out")

        def wait(eng, s, it, k):
            assert 1 <= k <= per[s]
            eng.wait_ge(s, it * per[s] + k)

        def mm3(o, st_hi, st_lo, mv_hi, mv_lo, first=True, last=True):
            nc.tensor.matmul(o, st_hi, mv_hi, start=first, stop=False)
            nc.tensor.matmul(o, st_hi, mv_lo, start=False, stop=False)
            return nc.tensor.matmul(o, st_lo, mv_hi, start=False, stop=last)

        A_JOBS = []
        for b in range(B):
            if b == 0:
                A_JOBS += [(0, "wvp", 0)]
            A_JOBS += [(b, "v", t) for t in range(3)]
            if b == 0:
                A_JOBS += [(0, "gate", 0), (0, "gate", 1), (0, "row", 0)]
            A_JOBS += [(b, "v", t) for t in range(3, T)] + [(b, "qk", j) for j in (4, 5, 6)] + [(b, "ctx", 0)]
            A_JOBS += [(b, "qk", 7), (b, "ctx", 1), (b, "ctx", 2), (b, "ctx", 3)]
            A_JOBS += [(b, "pv", i) for i in range(T)] + [(b, "f2", t) for t in range(T)]
        A_READ_OUT = {"v": vlo_ready, "qk": qk32_ready, "ctx": tanh_ready, "pv": o1_ready, "f2": t2_ready,
                      "wvp": wv_lo_ready, "gate": gate_copied, "row": rows_copied}
        T_JOBS = []
        for b in range(B):
            if b == 0:
                T_JOBS += [(0, "mod", 0)]
            T_JOBS += [(b, "h", r) for r in range(4)]
            if b == 0:
                T_JOBS += [(0, "mod", 1)]
            T_JOBS += [(b, "p", n) for n in range(2 * UNITS)] + [(b, "h", r) for r in range(4, 8)]
        T_READ_OUT = {"h": h32_ready, "p": ptlo_ready, "mod": mod_copied}

        def a_bank(b, kind, k):
            return a_ps[A_JOBS.index((b, kind, k)) % 2]

        def t_bank(b, kind, k):
            return t_ps[T_JOBS.index((b, kind, k)) % 2]

        def read_out(jobs, signals, job):
            n = jobs.index(job)
            if n < 2:
                return None
            b, kind, k = jobs[n - 2]
            s = signals[kind]
            return s, b * per.get(s, 0) + k + 1

        QK_JOBS = [(0, 0), (2, 0), (2, 1), (0, 1), (1, 0), (3, 0), (1, 1), (3, 1)]

        block = ctx.enter_context(nc.Block())

        @block.sync
        def _(sp):
            def load_x(h):
                sp.dma_start(x_all[:, h * TH:(h + 1) * TH, :], x_v[:, h * TH:(h + 1) * TH, :]).then_inc(x_in[h], 16)

            wa = w_attn.rearrange("(c p) n -> p c n", p=P)
            wm = wmod.rearrange("(c p) n -> p c n", p=P)
            sp.dma_start(cols_sb[:, :], cols).then_inc(cols_in, 16)
            load_x(0)
            sp.dma_start(wmod_raw[:, :, 0:2 * E], wm[:, :, 0:2 * E]).then_inc(wmod1_in, 16)
            sp.dma_start(wattn_raw[:, :, 0:2 * E], wa[:, :, 0:2 * E]).then_inc(wqk_in, 16)
            load_x(1)
            sp.dma_start(wvt_raw[:, :, :], wv_t.rearrange("(c p) n -> p c n", p=P)).then_inc(wvt_in, 16)
            sp.dma_start(wp_raw[:, :, :], wp.rearrange("(c p) n -> p c n", p=P)).then_inc(wp_in, 16)
            sp.dma_start(wattn_raw[:, :, 2 * E:3 * E], wa[:, :, 2 * E:3 * E]).then_inc(wv_in, 16)
            sp.dma_start(wmod_raw[:, :, 2 * E:6 * E], wm[:, :, 2 * E:6 * E]).then_inc(wmod2_in, 16)
            sp.dma_start(rows_raw[:, :], rows).then_inc(rows_in, 16)
            load_x(2)
            load_x(3)
            wait(sp, v_psum, 0, T)
            wait(sp, qk_psum, 0, 8)
            sp.dma_start(w1_raw[:, :, :], w1_t.rearrange("(c p) n -> p c n", p=P)).then_inc(w1_in, 16)
            sp.dma_start(w2_raw[:, :, :], w2_t.rearrange("(c p) n -> p c n", p=P)).then_inc(w2_in, 16)
            for b in range(B):
                for t in range(T):
                    wait(sp, y_ready, b, t + 1)
                    sp.dma_start(out_v[:, b * T + t, :], x_all[:, b * T + t, :]).then_inc(y_out, 16)
            sp.wait_ge(y_out, 16 * B * T)

        @block.gpsimd
        def _(pool):
            G = nc.gpsimd
            G.memset(ident[:, :], 0.0).then_inc(const_ready, 1)
            G.memset(ones_row[:, :], 1.0)
            G.memset(minus_half[:, :], -0.5).then_inc(const_ready, 1)
            pool.wait_ge(const_ready, 2)
            G.affine_select(out=ident[:, :], in_=ident[:, :], compare_op=ALU.not_equal, fill=1.0,
                            base=0, pattern=[[-1, P]], channel_multiplier=1).then_inc(ident_ready, 1)

            def inv_std(b, n):
                h = slice((n % 2) * TH, (n % 2 + 1) * TH)
                wait(pool, ve_ready, b, n + 1)
                G.tensor_tensor(rstd[:, h], ve[:, h], minus_half[:, :], ALU.pow).then_inc(rstd_ready, 1)

            def divide_by_sum(b, u):
                wait(pool, rinv_ready, b, u + 1)
                G.tensor_scalar(prob[:, u % 3, :], prob[:, u % 3, :], rinv[:, u:u + 1], 1.0,
                                ALU.mult, ALU.mult).then_inc(pnorm_ready, 1)

            def split_ffn(n):
                src, hi, lo, arrived = (w1_raw, w1_hi, w1_lo, w1_in) if n < 4 else (w2_raw, w2_hi, w2_lo, w2_in)
                src, hi, lo = (a[:, :, :].rearrange("p c n -> p (c n)")[:, (n % 4) * HALF:(n % 4 + 1) * HALF]
                               for a in (src, hi, lo))
                pool.wait_ge(arrived, 16)
                G.tensor_scalar(hi, src, 1.0, 1.0, ALU.mult, ALU.mult).then_inc(wffn_hi, 1)
                pool.wait_ge(wffn_hi, n + 1)
                G.tensor_tensor(lo, src, f(hi), ALU.subtract).then_inc(wffn_lo, 1)

            def attn_const(b, t):
                pool.wait_ge(consts_ready, 1)
                wait(pool, xn_ready, b, 1 + t // TH)
                xt = x_all[:, b * T + t, :]
                G.tensor_tensor(xt, xt, consts[:, b, 0, :], ALU.add).then_inc(xc_ready, 1)

            def attn_residual(b, t):
                wait(pool, o1_ready, b, t + 1)
                wait(pool, xc_ready, b, t + 1)
                xt = x_all[:, b * T + t, :]
                G.tensor_tensor(xt, xt, o1[:, t % 2, :], ALU.add).then_inc(x2_ready, 1)

            def gelu_high(b, n):
                wait(pool, gelu_ready, b, n + 1)
                G.tensor_scalar(gt_hi[:, n % HC, :], f32s[:, n % 3, :], 1.0, 1.0, ALU.mult, ALU.mult)\
                    .then_inc(ghi_ready, 1)

            def ffn_const(b, t):
                wait(pool, xn_ready, b, 3 + t // TH)
                xt = x_all[:, b * T + t, :]
                G.tensor_tensor(xt, xt, consts[:, b, 1, :], ALU.add).then_inc(x2c_ready, 1)

            def result(b, t):
                wait(pool, t2_ready, b, t + 1)
                wait(pool, x2c_ready, b, t + 1)
                xt = x_all[:, b * T + t, :]
                G.tensor_tensor(xt, xt, o1[:, t % 2, :], ALU.add).then_inc(y_ready, 1)

            inv_std(0, 0)
            inv_std(0, 1)
            for b in range(B):
                for s in range(UNITS):
                    if s < T:
                        divide_by_sum(b, s)
                    if b == 0 and s >= T:
                        split_ffn(s - T)
                    if s >= 10:
                        attn_const(b, s - 10)
                    if s >= 11:
                        attn_residual(b, s - 11)
                attn_const(b, 6)
                inv_std(b, 2)
                attn_residual(b, 5)
                attn_const(b, 7)
                attn_residual(b, 6)
                for n in range(HC):
                    gelu_high(b, n)
                    if n == 1:
                        attn_residual(b, 7)
                    if n == 4:
                        inv_std(b, 3)
                    if n >= 4:
                        ffn_const(b, n - 4)
                for t in range(TH):
                    result(b, t)
                for n in range(HC, 2 * HC):
                    gelu_high(b, n)
                    if n >= HC + 4:
                        ffn_const(b, n - HC)
                    if b + 1 < B and n == HC + 1:
                        inv_std(b + 1, 0)
                    if b + 1 < B and n == HC + 5:
                        inv_std(b + 1, 1)
                for t in range(TH, T):
                    result(b, t)

        @block.scalar
        def _(act):
            A = nc.scalar.activation
            act.wait_ge(cols_in, 16)
            A(exps[:, 0:EC * B], cols_sb[:, C_CT:C_CT + EC * B], ACT.Exp, scale=-1.0).then_inc(exps_ready, 1)
            act.wait_ge(lw_ready, 1)
            A(exps[:, EC * B:EC * B + 1], lw_arg[:, :], ACT.Exp, scale=-1.0).then_inc(exps_ready, 1)
            act.wait_ge(wqk_in, 16)
            A(wqk_hi[:, :, :], wattn_raw[:, :, 0:2 * E], ACT.Copy).then_inc(wqk_hi_ready, 1)

            def affine(b, r):
                wait(act, ht_psum, b, r + 1)
                if r >= 2 or b:
                    act.wait_ge(hlo_ready, b * 8 + r - 1)
                act.wait_ge(mod_ready, 1 + r // 4)
                v = 4 * (r // 4) + r % 2
                A(h32[:, r % 2, :], t_bank(b, "h", r)[:, :], ACT.Identity,
                  scale=modc[:, b, v + 2:v + 3], bias=modc[:, b, v:v + 1]).then_inc(h32_ready, 1)

            def qk_bias(b, j):
                m, h = QK_JOBS[j]
                wait(act, qk_psum, b, j + 1)
                if j >= 3:
                    wait(act, qklo_ready, b, j - 2)
                src = s_bank(j) if j < 4 else a_bank(b, "qk", j)[:, :]
                if m < 2:
                    a = A(f32s[:, j % 3, :], src, ACT.Identity, scale=QSCALE, bias=bq_scaled[:, m:m + 1])
                else:
                    a = A(f32s[:, j % 3, :], src, ACT.Identity, bias=cols_sb[:, C_BK + m - 2:C_BK + m - 1])
                a.then_inc(qk32_ready, 1)

            def v_high(b, t):
                wait(act, v_psum, b, t + 1)
                A(v_hi[:, t, :], a_bank(b, "v", t)[:, 0:NV], ACT.Copy).then_inc(vhi_ready, 1)

            def prob_high(b, u):
                for g in range(2):
                    wait(act, t_psum, b, 2 * u + g + 1)
                    if b == 0 and u == 0:
                        act.wait_ge(wv_lo_ready, 1)
                    A(pt_hi[:, (u // 2) % 2, 4 * g:4 * g + 4, (u % 2) * P:(u % 2 + 1) * P],
                      t_bank(b, "p", 2 * u + g)[:, :].rearrange("p (t n) -> p t n", n=P),
                      ACT.Copy).then_inc(pthi_ready, 1)

            def softmax_exp(b, u):
                wait(act, nmax_ready, b, u + 1)
                if u >= 3:
                    wait(act, t_psum, b, 2 * (u - 2))
                A(prob[:, u % 3, :], s_ps[u % 2][:, :], ACT.Exp, bias=nmax[:, u:u + 1],
                  accum_out=rsum[:, u:u + 1]).then_inc(exp_ready, 1)

            def cam_tanh(b, p):
                wait(act, ctx_psum, b, p + 1)
                if p >= 2:
                    wait(act, qplo_ready, b, p - 1)
                A(th[:, p % 2, :], a_bank(b, "ctx", p)[:, 0:2 * P], ACT.Tanh,
                  scale=cols_sb[:, C_GATE:C_GATE + 1], bias=gate_bias[:, :]).then_inc(tanh_ready, 1)

            def gelu(b, n):
                wait(act, f1_psum, b, n + 1)
                if n >= 3:
                    wait(act, glo_ready, b, n - 2)
                A(f32s[:, n % 3, :], s_bank(n % 4), ACT.Gelu,
                  bias=cols_sb[:, C_B1 + n % HC:C_B1 + n % HC + 1]).then_inc(gelu_ready, 1)

            affine(0, 0)
            affine(0, 1)
            for b in range(B):
                if b == 0:
                    act.wait_ge(wv_in, 16)
                    A(wv_hi[:, :, 0:DK], wattn_raw[:, :, 2 * E:2 * E + DK], ACT.Copy)
                    act.wait_ge(wvp_psum, 1)
                    A(wv_hi[:, :, DK:NV], a_bank(0, "wvp", 0)[:, :].rearrange("p (c n) -> p c n", c=EC), ACT.Copy)\
                        .then_inc(wv_hi_ready, 1)
                    affine(0, 2)
                    affine(0, 3)
                for j in range(4):
                    qk_bias(b, j)
                for s in range(UNITS + 2):
                    if s >= 2:
                        prob_high(b, s - 2)
                    if s == 0:
                        v_high(b, 0)
                        v_high(b, 1)
                    if s < UNITS:
                        softmax_exp(b, s)
                    if s == 0:
                        v_high(b, 2)
                        if b == 0:
                            for g in range(B):
                                act.wait_ge(gate_psum, g + 1)
                                A(gates[:, g, :, :], a_bank(0, "gate", g)[:, :].rearrange("p (v n) -> p v n", v=2),
                                  ACT.Copy, scale=2.0).then_inc(gate_copied, 1)
                            act.wait_ge(row_psum, 1)
                            A(consts[:, 0, :, :], a_bank(0, "row", 0)[:, :].rearrange("p (v n) -> p v n", v=2),
                              ACT.Copy).then_inc(rows_copied, 1)
                    if s == 1:
                        for t in (3, 4, 5):
                            v_high(b, t)
                    if s == 2:
                        v_high(b, 6)
                        v_high(b, 7)
                    if s == 3:
                        qk_bias(b, 4)
                        qk_bias(b, 5)
                    if s == 4:
                        qk_bias(b, 6)
                    if s == 6:
                        qk_bias(b, 7)
                    if s in (5, 7, 9, 11):
                        cam_tanh(b, (s - 5) // 2)
                affine(b, 4)
                affine(b, 5)
                for n in range(HC):
                    gelu(b, n)
                affine(b, 6)
                affine(b, 7)
                for n in range(HC, 2 * HC):
                    gelu(b, n)
                    if b + 1 < B and n == HC + 5:
                        affine(b + 1, 0)
                        affine(b + 1, 1)
                if b + 1 < B:
                    affine(b + 1, 2)
                    affine(b + 1, 3)

        @block.vector
        def _(dve):
            V = nc.vector
            dve.wait_ge(cols_in, 16)
            V.tensor_scalar(lw_arg[:, :], cols_sb[:, C_W1:C_W1 + 1], DEPTH, cols_sb[:, C_W0:C_W0 + 1],
                            ALU.mult, ALU.add).then_inc(lw_ready, 1)
            V.tensor_scalar(bq_scaled[:, :], cols_sb[:, C_BQ:C_BQ + 2], QSCALE, None, ALU.mult)
            V.tensor_tensor(gate_bias[:, :], cols_sb[:, C_BVC:C_BVC + 1], cols_sb[:, C_GATE:C_GATE + 1], ALU.mult)
            V.tensor_copy(bvb[:, :, :], cols_sb[:, C_BV:C_BV + 2].rearrange("p (c a) -> p c a", a=1)
                          .to_broadcast([P, EC, P])).then_inc(bias_ready, 1)
            dve.wait_ge(exps_ready, 2)
            V.tensor_scalar(exps[:, :], exps[:, :], 1.0, None, ALU.add).then_inc(plus1_ready, 1)
            dve.wait_ge(plus1_ready, 1)
            V.reciprocal(exps[:, :], exps[:, :]).then_inc(recip_ready, 1)
            dve.wait_ge(recip_ready, 1)
            V.tensor_tensor(sct[:, :, :], cols_sb[:, C_CT:C_CT + EC * B].rearrange("p (c b) -> p c b", b=B),
                            exps[:, 0:EC * B].rearrange("p (c b) -> p c b", b=B), ALU.mult).then_inc(sct_ready, 1)
            V.tensor_scalar(lw_scaled[:, :], exps[:, EC * B:EC * B + 1], QSCALE, None, ALU.mult)
            dve.wait_ge(sct_ready, 1)
            V.tensor_copy(scb[:, :, :, :].rearrange("p c b n -> p (c b) n"),
                          sct[:, :, :].rearrange("p c b -> p (c b)").rearrange("p (m a) -> p m a", a=1)
                          .to_broadcast([P, EC * B, P])).then_inc(silu_ready, 1)

            def norm_stats(b, n):
                h = n % 2
                if n < 2:
                    dve.wait_ge(x_in[2 * b + h], 16)
                for t in range(h * TH, (h + 1) * TH):
                    if n >= 2:
                        wait(dve, x2_ready, b, t + 1)
                    last = V.bn_stats(bst[:, t, :], x_all[:, b * T + t, :])
                last.then_inc(bst_ready, 1)
                wait(dve, bst_ready, b, n + 1)
                for t in range(h * TH, (h + 1) * TH):
                    last = V.bn_aggr(mv[:, t, :], bst[:, t, :])
                last.then_inc(mv_ready, 1)
                wait(dve, mv_ready, b, n + 1)
                V.tensor_scalar(ve[:, h * TH:(h + 1) * TH], mv[:, h * TH:(h + 1) * TH, 1], EPS, None, ALU.add)\
                    .then_inc(ve_ready, 1)

            def norm_apply(b, n):
                h = n % 2
                wait(dve, rstd_ready, b, n + 1)
                if n or b:
                    dve.wait_ge(ht_psum, b * 8 + 2 * n)
                for t in range(TH):
                    j = h * TH + t
                    last = V.tensor_scalar(xn[:, t, :], x_all[:, b * T + j, :], mv[:, j, 0:1], rstd[:, j:j + 1],
                                           ALU.subtract, ALU.mult)
                last.then_inc(xn_ready, 1)

            def h_split(b, r):
                h, c = (r // 2) % 2, r % 2
                wait(dve, h32_ready, b, r + 1)
                if b == 0 and r == 4:
                    dve.wait_ge(wffn_lo, 8)
                dst = (slice(None), c, slice(h * HALF, (h + 1) * HALF))
                V.tensor_copy(ht_hi[dst], h32[:, r % 2, :]).then_inc(hhi_ready, 1)
                wait(dve, hhi_ready, b, r + 1)
                V.tensor_tensor(ht_lo[dst], h32[:, r % 2, :], f(ht_hi[dst]), ALU.subtract).then_inc(hlo_ready, 1)

            def qk_split(b, j):
                m, h = QK_JOBS[j]
                hi, lo = (q_hi, q_lo) if m < 2 else (k_hi, k_lo)
                dst = (slice(None), m % 2, slice(h * HALF, (h + 1) * HALF))
                wait(dve, qk32_ready, b, j + 1)
                V.tensor_copy(hi[dst], f32s[:, j % 3, :]).then_inc(qkhi_ready, 1)
                wait(dve, qkhi_ready, b, j + 1)
                V.tensor_tensor(lo[dst], f32s[:, j % 3, :], f(hi[dst]), ALU.subtract).then_inc(qklo_ready, 1)

            def v_low(b, t):
                wait(dve, vhi_ready, b, t + 1)
                V.tensor_tensor(v_lo[:, t, :], a_bank(b, "v", t)[:, 0:NV], f(v_hi[:, t, :]), ALU.subtract)\
                    .then_inc(vlo_ready, 1)

            def q_update(b, p):
                dst = (slice(None), 0, slice(2 * P * p, 2 * P * (p + 1)))
                t = th[:, p % 2, :]
                wait(dve, tanh_ready, b, p + 1)
                V.scalar_tensor_tensor(t, t, lw_scaled[:, :], f(q_lo[dst]), ALU.mult, ALU.add).then_inc(qcam_ready, 1)
                wait(dve, qcam_ready, b, 2 * p + 1)
                V.tensor_tensor(t, t, f(q_hi[dst]), ALU.add).then_inc(qcam_ready, 1)
                wait(dve, qcam_ready, b, 2 * p + 2)
                V.tensor_copy(q_hi[dst], t).then_inc(qphi_ready, 1)
                wait(dve, qphi_ready, b, p + 1)
                V.tensor_tensor(q_lo[dst], t, f(q_hi[dst]), ALU.subtract).then_inc(qplo_ready, 1)

            def prob_low(b, u):
                for g in range(2):
                    wait(dve, pthi_ready, b, 2 * u + g + 1)
                    dst = (slice(None), (u // 2) % 2, slice(4 * g, 4 * g + 4), slice((u % 2) * P, (u % 2 + 1) * P))
                    V.tensor_tensor(pt_lo[dst], t_bank(b, "p", 2 * u + g)[:, :].rearrange("p (t n) -> p t n", n=P),
                                    f(pt_hi[dst]), ALU.subtract).then_inc(ptlo_ready, 1)

            def row_max(b, u):
                wait(dve, s_psum, b, u + 1)
                V.tensor_reduce(nmax[:, u:u + 1], s_ps[u % 2][:, :], AX.X, ALU.max, negate=True).then_inc(nmax_ready, 1)

            def row_recip(b, u):
                wait(dve, exp_ready, b, u + 1)
                V.reciprocal(rinv[:, u:u + 1], rsum[:, u:u + 1]).then_inc(rinv_ready, 1)

            def attn_gated(b, i):
                wait(dve, pv_psum, b, i + 1)
                if i >= 2:
                    wait(dve, x2_ready, b, i - 1)
                elif b:
                    wait(dve, y_ready, b - 1, T - 1 + i)
                V.scalar_tensor_tensor(o1[:, i % 2, :], a_bank(b, "pv", i)[:, 0:E], rinv[:, T + i:T + i + 1],
                                       gates[:, b, 0, :], ALU.mult, ALU.mult).then_inc(o1_ready, 1)

            def ffn_gated(b, i):
                wait(dve, f2_psum, b, i + 1)
                if i >= 2:
                    wait(dve, y_ready, b, i - 1)
                else:
                    wait(dve, x2_ready, b, T - 1 + i)
                V.tensor_tensor(o1[:, i % 2, :], a_bank(b, "f2", i)[:, 0:E], gates[:, b, 1, :], ALU.mult)\
                    .then_inc(t2_ready, 1)

            def gelu_low(b, n):
                wait(dve, ghi_ready, b, n + 1)
                V.tensor_tensor(gt_lo[:, n % HC, :], f32s[:, n % 3, :], f(gt_hi[:, n % HC, :]), ALU.subtract)\
                    .then_inc(glo_ready, 1)

            def mod_columns(n):
                dve.wait_ge((mod1_psum, mod2_psum)[n], 1)
                V.tensor_copy(modc[:, :, 4 * n:4 * n + 4],
                              t_bank(0, "mod", n)[:, 0:8].rearrange("p (b v) -> p b v", b=B)).then_inc(mod_copied, 1)
                dve.wait_ge(mod_copied, n + 1)
                c = modc[:, :, 4 * n + 2:4 * n + 4]
                V.tensor_scalar(c, c, 1.0, None, ALU.add).then_inc(mod_ready, 1)

            def finish_gates():
                g2 = gates[:, :, :, :].rearrange("p b v n -> p (b v n)")
                tmp = f32s[:, 0:2, :].rearrange("p a n -> p (a n)")
                dve.wait_ge(gate_copied, 2)
                V.scalar_tensor_tensor(tmp, g2, -1.0, g2, ALU.mult, ALU.max).then_inc(gate_abs, 1)
                dve.wait_ge(gate_abs, 1)
                V.tensor_scalar(g2, g2, 0.0, -0.5, ALU.is_ge, ALU.add).then_inc(gate_sign, 1)
                dve.wait_ge(gate_sign, 1)
                V.scalar_tensor_tensor(g2, tmp, 0.5, g2, ALU.max, ALU.mult).then_inc(gates_ready, 1)

            def finish_consts():
                dve.wait_ge(rows_copied, 1)
                dve.wait_ge(gates_ready, 1)
                V.tensor_tensor(consts[:, 1, :, :], consts[:, 0, :, :], gates[:, 1, :, :], ALU.mult).then_inc(const_other, 1)
                dve.wait_ge(const_other, 1)
                V.tensor_tensor(consts[:, 0, :, :], consts[:, 0, :, :], gates[:, 0, :, :], ALU.mult).then_inc(consts_ready, 1)

            norm_stats(0, 0)
            mod_columns(0)
            norm_apply(0, 0)
            norm_stats(0, 1)
            h_split(0, 0)
            h_split(0, 1)
            dve.wait_ge(wqk_hi_ready, 1)
            V.tensor_tensor(wqk_lo[:, :, :], wattn_raw[:, :, 0:2 * E], f(wqk_hi[:, :, :]), ALU.subtract)\
                .then_inc(wqk_lo_ready, 1)
            norm_apply(0, 1)
            for b in range(B):
                if b == 0:
                    dve.wait_ge(wv_hi_ready, 1)
                    V.tensor_tensor(wv_lo[:, :, 0:DK], wattn_raw[:, :, 2 * E:2 * E + DK], f(wv_hi[:, :, 0:DK]), ALU.subtract)
                    V.tensor_tensor(wv_lo[:, :, DK:NV], a_bank(0, "wvp", 0)[:, :].rearrange("p (c n) -> p c n", c=EC),
                                    f(wv_hi[:, :, DK:NV]), ALU.subtract).then_inc(wv_lo_ready, 1)
                    h_split(0, 2)
                    h_split(0, 3)
                for j in range(4):
                    qk_split(b, j)
                for s in range(UNITS + 2):
                    if s < UNITS:
                        row_max(b, s)
                    if s == 0:
                        v_low(b, 0)
                    if s == UNITS:
                        norm_apply(b, 2)
                    if s >= 2:
                        prob_low(b, s - 2)
                    if s < UNITS:
                        row_recip(b, s)
                    if s >= T + 3:
                        attn_gated(b, s - T - 3)
                    if s == 0:
                        v_low(b, 1)
                        v_low(b, 2)
                    if s == 1:
                        if b == 0:
                            mod_columns(1)
                        for t in (3, 4, 5):
                            v_low(b, t)
                    if s == 2:
                        v_low(b, 6)
                        v_low(b, 7)
                    if s == 3:
                        qk_split(b, 4)
                        qk_split(b, 5)
                    if s == 4:
                        qk_split(b, 6)
                    if s == 6:
                        qk_split(b, 7)
                    if s in (5, 7, 9, 11):
                        q_update(b, (s - 5) // 2)
                    if b == 0 and s == 8:
                        finish_gates()
                    if b == 0 and s == 10:
                        finish_consts()
                    if s == UNITS - 1:
                        norm_stats(b, 2)
                h_split(b, 4)
                h_split(b, 5)
                for n in range(HC):
                    gelu_low(b, n)
                    if n == 1:
                        attn_gated(b, T - 1)
                    if n == 2:
                        norm_stats(b, 3)
                    if n == 5:
                        norm_apply(b, 3)
                ffn_gated(b, 0)
                h_split(b, 6)
                h_split(b, 7)
                for t in range(1, TH):
                    ffn_gated(b, t)
                for n in range(HC, 2 * HC):
                    gelu_low(b, n)
                    if b + 1 < B:
                        if n == HC:
                            norm_stats(b + 1, 0)
                        if n == HC + 3:
                            norm_apply(b + 1, 0)
                        if n == HC + 4:
                            norm_stats(b + 1, 1)
                if b + 1 < B:
                    h_split(b + 1, 0)
                    h_split(b + 1, 1)
                    norm_apply(b + 1, 1)
                ffn_gated(b, TH)
                if b + 1 < B:
                    h_split(b + 1, 2)
                    h_split(b + 1, 3)
                for t in range(TH + 1, T):
                    ffn_gated(b, t)

        @block.tensor
        def _(pe):
            M = nc.tensor.matmul

            def a_free(b, kind, k):
                if (w := read_out(A_JOBS, A_READ_OUT, (b, kind, k))) is not None:
                    pe.wait_ge(*w)

            def t_free(b, kind, k):
                if (w := read_out(T_JOBS, T_READ_OUT, (b, kind, k))) is not None:
                    pe.wait_ge(*w)

            def modulation(n):
                pe.wait_ge((wmod1_in, wmod2_in)[n], 16)
                pe.wait_ge(sct_ready, 1)
                t_free(0, "mod", n)
                o = t_bank(0, "mod", n)[:, 0:8].rearrange("p (b v) -> p b v", b=B)
                for v in range(4):
                    col = 3 * n * E + v * P
                    for k in range(EC):
                        last = M(o[:, :, v], wmod_raw[:, k, col:col + P], sct[:, k, :], start=k == 0, stop=k == EC - 1)
                last.then_inc((mod1_psum, mod2_psum)[n], 1)

            def gate_rows(b):
                pe.wait_ge(wmod2_in, 16)
                pe.wait_ge(silu_ready, 1)
                a_free(0, "gate", b)
                for v, col in enumerate((2 * E, 5 * E)):
                    for k in range(EC):
                        last = M(a_bank(0, "gate", b)[:, v * E:(v + 1) * E], scb[:, k, b, :], wmod_raw[:, k, col:col + E],
                                 start=k == 0, stop=k == EC - 1)
                last.then_inc(gate_psum, 1)

            def fold_projection():
                pe.wait_ge(wvt_in, 16)
                pe.wait_ge(wp_in, 16)
                o = a_bank(0, "wvp", 0)
                for m in range(EC):
                    for k in range(EC):
                        last = M(o[:, m * E:(m + 1) * E], wvt_raw[:, k, m * P:(m + 1) * P], wp_raw[:, k, :],
                                 start=k == 0, stop=k == EC - 1)
                last.then_inc(wvp_psum, 1)

            def bias_rows():
                pe.wait_ge(rows_in, 16)
                pe.wait_ge(const_ready, 2)
                pe.wait_ge(bias_ready, 1)
                a_free(0, "row", 0)
                o = a_bank(0, "row", 0)
                for k in range(EC):
                    M(o[:, 0:E], bvb[:, k, :], wp_raw[:, k, :], start=k == 0, stop=False)
                M(o[:, 0:E], ones_row[0:1, :], rows_raw[0:1, 0:E], start=False, stop=True)
                M(o[:, E:2 * E], ones_row[0:1, :], rows_raw[0:1, E:2 * E], start=True, stop=True).then_inc(row_psum, 1)

            def h_transpose(b, r):
                wait(pe, xn_ready, b, r // 2 + 1)
                t_free(b, "h", r)
                c = r % 2
                for t in range(TH):
                    last = nc.tensor.transpose(t_bank(b, "h", r)[:, t * P:(t + 1) * P], xn[:, t, c * P:(c + 1) * P],
                                               ident[:, :])
                last.then_inc(ht_psum, 1)

            def qk_project(b, j):
                m, h = QK_JOBS[j]
                if j < 4:
                    wait(pe, hlo_ready, b, 2 * h + 2)
                    if b:
                        wait(pe, gelu_ready, b - 1, 2 * HC - 3 + j)
                    o = s_bank(j)
                else:
                    a_free(b, "qk", j)
                    o = a_bank(b, "qk", j)[:, :]
                n = slice(h * HALF, (h + 1) * HALF)
                for k in range(EC):
                    last = mm3(o, wqk_hi[:, k, m * P:(m + 1) * P], wqk_lo[:, k, m * P:(m + 1) * P],
                               ht_hi[:, k, n], ht_lo[:, k, n], k == 0, k == EC - 1)
                last.then_inc(qk_psum, 1)

            def v_project(b, t):
                wait(pe, hlo_ready, b, 2 * (t // TH) + 2)
                a_free(b, "v", t)
                n = slice(t * P, (t + 1) * P)
                for k in range(EC):
                    last = mm3(a_bank(b, "v", t)[:, 0:NV], ht_hi[:, k, n], ht_lo[:, k, n], wv_hi[:, k, :],
                               wv_lo[:, k, :], k == 0, k == EC - 1)
                last.then_inc(v_psum, 1)

            def scores(b, u):
                n = slice((u % T) * P, (u % T + 1) * P)
                if u == 0:
                    wait(pe, qklo_ready, b, 3)
                if u == 2:
                    wait(pe, qklo_ready, b, 4)
                if u == 1:
                    wait(pe, qk32_ready, b, 4)
                if u >= 2:
                    wait(pe, exp_ready, b, u - 1)
                if u == T:
                    wait(pe, qklo_ready, b, 8)
                if u >= T and u % 2 == 0:
                    wait(pe, qplo_ready, b, (u - T) // 2 + 1)
                chunks = 1 if u < T else EC
                for g in range(2):
                    keys = slice(g * HALF, (g + 1) * HALF)
                    for k in range(chunks):
                        last = mm3(s_ps[u % 2][:, keys], q_hi[:, k, n], q_lo[:, k, n], k_hi[:, k, keys],
                                   k_lo[:, k, keys], k == 0, k == chunks - 1)
                last.then_inc(s_psum, 1)

            def transpose_probs(b, u):
                wait(pe, pnorm_ready if u < T else exp_ready, b, u + 1)
                for g in range(2):
                    t_free(b, "p", 2 * u + g)
                    for t in range(4):
                        c = (4 * g + t) * P
                        last = nc.tensor.transpose(t_bank(b, "p", 2 * u + g)[:, t * P:(t + 1) * P],
                                                   prob[:, u % 3, c:c + P], ident[:, :])
                    last.then_inc(t_psum, 1)

            def cam_context(b, p):
                if p == 0:
                    wait(pe, vlo_ready, b, T)
                wait(pe, ptlo_ready, b, 4 * p + 4)
                a_free(b, "ctx", p)
                for t in range(T):
                    last = mm3(a_bank(b, "ctx", p)[:, 0:2 * P], v_hi[:, t, 0:DK], v_lo[:, t, 0:DK],
                               pt_hi[:, p % 2, t, :], pt_lo[:, p % 2, t, :], t == 0, t == T - 1)
                last.then_inc(ctx_psum, 1)

            def attend(b, i):
                u = T + i
                wait(pe, ptlo_ready, b, 2 * u + 2)
                a_free(b, "pv", i)
                n = slice((u % 2) * P, (u % 2 + 1) * P)
                for t in range(T):
                    last = mm3(a_bank(b, "pv", i)[:, 0:E], pt_hi[:, (u // 2) % 2, t, n], pt_lo[:, (u // 2) % 2, t, n],
                               v_hi[:, t, DK:NV], v_lo[:, t, DK:NV], t == 0, t == T - 1)
                last.then_inc(pv_psum, 1)

            def ffn_up(b, n):
                h, c = n // HC, n % HC
                if c == 0:
                    wait(pe, hlo_ready, b, 6 + 2 * h)
                if n < 4:
                    wait(pe, exp_ready, b, UNITS - 1 + n // 2)
                else:
                    wait(pe, gelu_ready, b, n - 3)
                tokens = slice(h * HALF, (h + 1) * HALF)
                for k in range(EC):
                    last = mm3(s_bank(n % 4), w1_hi[:, k, c * P:(c + 1) * P], w1_lo[:, k, c * P:(c + 1) * P],
                               ht_hi[:, k, tokens], ht_lo[:, k, tokens], k == 0, k == EC - 1)
                last.then_inc(f1_psum, 1)

            def ffn_down(b, i):
                a_free(b, "f2", i)
                n = slice((i % TH) * P, (i % TH + 1) * P)
                for c in range(HC):
                    if i % TH == 0:
                        wait(pe, glo_ready, b, (i // TH) * HC + c + 1)
                    last = mm3(a_bank(b, "f2", i)[:, 0:E], gt_hi[:, c, n], gt_lo[:, c, n], w2_hi[:, c, :],
                               w2_lo[:, c, :], c == 0, c == HC - 1)
                last.then_inc(f2_psum, 1)

            modulation(0)
            pe.wait_ge(ident_ready, 1)
            h_transpose(0, 0)
            h_transpose(0, 1)
            fold_projection()
            pe.wait_ge(wqk_lo_ready, 1)
            for b in range(B):
                qk_project(b, 0)
                qk_project(b, 1)
                if b == 0:
                    h_transpose(0, 2)
                    h_transpose(0, 3)
                qk_project(b, 2)
                qk_project(b, 3)
                if b == 0:
                    pe.wait_ge(wv_lo_ready, 1)
                v_project(b, 0)
                v_project(b, 1)
                for s in range(UNITS + 2):
                    if s < UNITS:
                        scores(b, s)
                    if s >= 2:
                        transpose_probs(b, s - 2)
                    if s == 0:
                        v_project(b, 2)
                        if b == 0:
                            gate_rows(0)
                            gate_rows(1)
                            bias_rows()
                            modulation(1)
                    if s == 1:
                        for t in (3, 4, 5):
                            v_project(b, t)
                    if s == 2:
                        v_project(b, 6)
                        v_project(b, 7)
                    if s == 3:
                        qk_project(b, 4)
                        qk_project(b, 5)
                    if s == 4:
                        qk_project(b, 6)
                    if s == 6:
                        qk_project(b, 7)
                    if s in (5, 7, 9, 11):
                        cam_context(b, (s - 5) // 2)
                    if s >= T + 3:
                        attend(b, s - T - 3)
                h_transpose(b, 4)
                h_transpose(b, 5)
                if b == 0:
                    pe.wait_ge(wffn_lo, 8)
                for n in range(HC):
                    ffn_up(b, n)
                    if n == 1:
                        attend(b, T - 1)
                ffn_down(b, 0)
                h_transpose(b, 6)
                h_transpose(b, 7)
                for i in range(1, TH):
                    ffn_down(b, i)
                for n in range(HC, 2 * HC):
                    ffn_up(b, n)
                    if b + 1 < B and n == HC + 5:
                        h_transpose(b + 1, 0)
                        h_transpose(b + 1, 1)
                ffn_down(b, TH)
                if b + 1 < B:
                    h_transpose(b + 1, 2)
                    h_transpose(b + 1, 3)
                for i in range(TH + 1, T):
                    ffn_down(b, i)


def kernel(L0_attn_hidden_states, L0_attn_c_attn_w, L0_attn_c_attn_b, L0_attn_c_proj_w, L0_attn_c_proj_b,
           L0_attn_cam_gate, L0_attn_cam_w0, L0_attn_cam_w1, L0_ffn_proj1, L0_ffn_proj1_bias, L0_ffn_proj2,
           L0_ffn_proj2_bias, L0_ffn_gate_w, L0_c, L0_wmod):
    import numpy as np
    import concourse.bacc as bacc
    from concourse.bass_utils import run_bass_kernel_spmd

    def columns(v):
        return np.asarray(v).reshape(-1, P).T

    w_attn, b_attn = np.asarray(L0_attn_c_attn_w), np.asarray(L0_attn_c_attn_b)
    ct = np.asarray(L0_c).T.reshape(EC, P, B).transpose(1, 0, 2).reshape(P, EC * B)
    cols = np.concatenate([
        ct, columns(b_attn[0:E]), columns(b_attn[E:2 * E]), columns(b_attn[2 * E:2 * E + DK]), columns(b_attn[2 * E:]),
        columns(L0_attn_cam_gate), columns(L0_ffn_proj1_bias),
        np.broadcast_to(np.asarray(L0_attn_cam_w0), (P, 1)), np.broadcast_to(np.asarray(L0_attn_cam_w1), (P, 1))], axis=1)
    rows = np.concatenate([np.asarray(L0_attn_c_proj_b), np.asarray(L0_ffn_proj2_bias)]).reshape(1, 2 * E)
    arrays = {
        "x": np.asarray(L0_attn_hidden_states),
        "cols": cols,
        "wmod": np.asarray(L0_wmod),
        "w_attn": w_attn,
        "wv_t": w_attn[:, 2 * E:].T,
        "wp": np.asarray(L0_attn_c_proj_w),
        "rows": rows,
        "w1_t": np.asarray(L0_ffn_proj1).T,
        "w2_t": np.asarray(L0_ffn_proj2).T,
    }
    arrays = {n: np.ascontiguousarray(a) for n, a in arrays.items()}
    nc = bacc.Bacc("TRN2", target_bir_lowering=False, num_devices=1)
    args = [nc.dram_tensor(n, a.shape, mybir.dt.from_np(a.dtype), kind="ExternalInput").ap() for n, a in arrays.items()]
    out = nc.dram_tensor("out", (B, S, E), F32, kind="ExternalOutput").ap()
    adaln_block_kernel(nc, *args, out)
    r = run_bass_kernel_spmd(nc, [arrays], core_ids=[0])
    return r.results[0]["out"]
```

```python
import concourse.bass as bass
from concourse import mybir
from contextlib import ExitStack

F32 = mybir.dt.float32
F32R = mybir.dt.float32r
ACT = mybir.ActivationFunctionType
ALU = mybir.AluOpType
AX = mybir.AxisListType

P = 128
B, S, E, H = 2, 1024, 256, 1024
DK = 128
EC, HC = E // P, H // P
T = S // P
HALF = 512
TH = HALF // P
QSCALE = 0.25
EPS = 1e-5
DEPTH = 0.5
NV = DK + E
UNITS = 2 * T

C_CT, C_BQ, C_BK, C_BVC, C_BV, C_GATE, C_B1, C_W0, C_W1 = 0, 4, 6, 8, 9, 11, 12, 20, 21
NCOLS = 22


def adaln_block_kernel(nc, x, cols, wmod, w_attn, wv_t, wp, rows, w1_t, w2_t, out):
    x_v = x.rearrange("b (t p) e -> p (b t) e", p=P)
    out_v = out.rearrange("b (t p) e -> p (b t) e", p=P)

    ctx = ExitStack()
    raw, raw_ffn = ExitStack(), ExitStack()
    with ctx:
        def sb(name, shape, dt=F32, scope=ctx):
            return scope.enter_context(nc.sbuf_tensor(name, shape, dt))

        def sem(name):
            return ctx.enter_context(nc.semaphore(name))

        x_all = sb("x_all", [P, B * T, E])
        ident = sb("ident", [P, P])
        cols_sb = sb("cols_sb", [P, NCOLS])
        exps = sb("exps", [P, EC * B + 1])
        sct = sb("sct", [P, EC, B])
        lw_arg = sb("lw_arg", [P, 1])
        lw_scaled = sb("lw_scaled", [P, 1])
        bq_scaled = sb("bq_scaled", [P, EC])
        gate_bias = sb("gate_bias", [P, 1])
        minus_half = sb("minus_half", [P, TH])
        modc = sb("modc", [P, B, 8])
        gates = sb("gates", [P, B, 2, E])
        consts = sb("consts", [P, B, 2, E])
        wqk_hi, wqk_lo = (sb(f"wqk_{n}", [P, EC, 2 * E], F32R) for n in ("hi", "lo"))
        wv_hi, wv_lo = (sb(f"wv_{n}", [P, EC, NV], F32R) for n in ("hi", "lo"))
        w1_hi, w1_lo = (sb(f"w1_{n}", [P, EC, H], F32R) for n in ("hi", "lo"))
        w2_hi, w2_lo = (sb(f"w2_{n}", [P, HC, E], F32R) for n in ("hi", "lo"))
        bst = sb("bst", [P, T, 6])
        mv = sb("mv", [P, T, 2])
        ve = sb("ve", [P, T])
        rstd = sb("rstd", [P, T])
        xn = sb("xn", [P, TH, E])
        h32 = sb("h32", [P, 2, HALF])
        f32s = sb("f32s", [P, 3, HALF])
        q_hi, q_lo = (sb(f"q_{n}", [P, EC, S], F32R) for n in ("hi", "lo"))
        k_hi, k_lo = (sb(f"k_{n}", [P, EC, S], F32R) for n in ("hi", "lo"))
        v_hi, v_lo = (sb(f"v_{n}", [P, T, NV], F32R) for n in ("hi", "lo"))
        nmax = sb("nmax", [P, UNITS])
        rsum = sb("rsum", [P, UNITS])
        rinv = sb("rinv", [P, UNITS])
        th = sb("th", [P, 2, 2 * P])
        o1 = sb("o1", [P, 2, E])
        prob = sb("prob", [P, 3, S])

        with raw_ffn:
            w1_raw = sb("w1_raw", [P, EC, H], scope=raw_ffn)
            w2_raw = sb("w2_raw", [P, HC, E], scope=raw_ffn)
        ht_hi, ht_lo = (sb(f"ht_{n}", [P, EC, S], F32R) for n in ("hi", "lo"))

        with raw:
            wattn_raw = sb("wattn_raw", [P, EC, 3 * E], scope=raw)
            wvt_raw = sb("wvt_raw", [P, EC, E], scope=raw)
            wp_raw = sb("wp_raw", [P, EC, E], scope=raw)
            scb = sb("scb", [P, EC, B, P // B], scope=raw)
            bvb = sb("bvb", [P, EC, P], scope=raw)
            sb("raw_gap0", [P, 8 * P], scope=raw)
            wmod1_raw = sb("wmod1_raw", [P, EC, 2 * E], scope=raw)
            sb("raw_gap1", [P, EC, 2 * E], scope=raw)
            wmod2_raw = sb("wmod2_raw", [P, EC, 4 * E], scope=raw)
        pt_hi, pt_lo = (sb(f"pt_{n}", [P, 2, T, 2 * P], F32R) for n in ("hi", "lo"))
        gt_hi, gt_lo = (a[:, :, :, :].rearrange("p a t n -> p (a t n)")
                        .rearrange("p (h n) -> p h n", n=HALF) for a in (pt_hi, pt_lo))

        s_ps = [ctx.enter_context(nc.psum_tensor(f"s_ps{i}", [P, 2 * HALF], F32)) for i in range(2)]
        t_ps = [ctx.enter_context(nc.psum_tensor(f"t_ps{i}", [P, HALF], F32)) for i in range(2)]
        a_ps = [ctx.enter_context(nc.psum_tensor(f"a_ps{i}", [P, HALF], F32)) for i in range(2)]

        def s_bank(k):
            return s_ps[k // 2][:, (k % 2) * HALF:(k % 2 + 1) * HALF]

        def f(ap):
            return ap.bitcast(F32)

        cols_in, wmod1_in, wmod2_in, wqk_in, wv_in, wvt_in, wp_in, rows_in, w1_in, w2_in = (
            sem(n) for n in ("cols_in", "wmod1_in", "wmod2_in", "wqk_in", "wv_in", "wvt_in", "wp_in", "rows_in",
                             "w1_in", "w2_in"))
        x_in = [sem(f"x_in{i}") for i in range(2 * B)]
        const_ready, ident_ready, bias_ready, lw_ready, exps_ready, plus1_ready, recip_ready, sct_ready, silu_ready, \
            mod1_psum, mod2_psum, mod_copied, mod_ready, gate_psum, gate_copied, gates_spread, gate_abs, gate_sign, gates_ready, \
            wvp_psum, row_psum, row_added, const_other, consts_ready, wqk_hi_ready, wqk_lo_ready, \
            wv_hi_ready, wv_lo_ready, wffn_hi, wffn_lo = (
                sem(n) for n in ("const_ready", "ident_ready", "bias_ready", "lw_ready", "exps_ready", "plus1_ready",
                                 "recip_ready", "sct_ready", "silu_ready", "mod1_psum", "mod2_psum", "mod_copied",
                                 "mod_ready", "gate_psum", "gate_copied", "gates_spread", "gate_abs", "gate_sign", "gates_ready",
                                 "wvp_psum", "row_psum", "row_added", "const_other", "consts_ready",
                                 "wqk_hi_ready", "wqk_lo_ready", "wv_hi_ready", "wv_lo_ready", "wffn_hi", "wffn_lo"))

        per = {}

        def lsem(name, n):
            s = sem(name)
            per[s] = n
            return s

        bst_ready = lsem("bst_ready", 4)
        mv_ready = lsem("mv_ready", 4)
        ve_ready = lsem("ve_ready", 4)
        rstd_ready = lsem("rstd_ready", 4)
        xn_ready = lsem("xn_ready", 4)
        ht_psum = lsem("ht_psum", 8)
        h32_ready = lsem("h32_ready", 8)
        hhi_ready = lsem("hhi_ready", 8)
        hlo_ready = lsem("hlo_ready", 8)
        qk_psum = lsem("qk_psum", 8)
        qk32_ready = lsem("qk32_ready", 8)
        qkhi_ready = lsem("qkhi_ready", 8)
        qklo_ready = lsem("qklo_ready", 8)
        v_psum = lsem("v_psum", T)
        vhi_ready = lsem("vhi_ready", T)
        vlo_ready = lsem("vlo_ready", T)
        s_psum = lsem("s_psum", UNITS)
        nmax_ready = lsem("nmax_ready", UNITS)
        exp_ready = lsem("exp_ready", UNITS)
        rinv_ready = lsem("rinv_ready", UNITS)
        pnorm_ready = lsem("pnorm_ready", T)
        t_psum = lsem("t_psum", 2 * UNITS)
        pthi_ready = lsem("pthi_ready", 2 * UNITS)
        ptlo_ready = lsem("ptlo_ready", 2 * UNITS)
        ctx_psum = lsem("ctx_psum", T // 2)
        tanh_ready = lsem("tanh_ready", T // 2)
        qcam_ready = lsem("qcam_ready", T)
        qphi_ready = lsem("qphi_ready", T // 2)
        qplo_ready = lsem("qplo_ready", T // 2)
        pv_psum = lsem("pv_psum", T)
        o1_ready = lsem("o1_ready", T)
        xc_ready = lsem("xc_ready", T)
        x2_ready = lsem("x2_ready", T)
        x2c_ready = lsem("x2c_ready", T)
        f1_psum = lsem("f1_psum", 2 * HC)
        gelu_ready = lsem("gelu_ready", 2 * HC)
        ghi_ready = lsem("ghi_ready", 2 * HC)
        glo_ready = lsem("glo_ready", 2 * HC)
        f2_psum = lsem("f2_psum", T)
        t2_ready = lsem("t2_ready", T)
        y_ready = lsem("y_ready", T)
        y_out = sem("y_out")

        def wait(eng, s, it, k):
            assert 1 <= k <= per[s]
            eng.wait_ge(s, it * per[s] + k)

        def mm3(o, st_hi, st_lo, mv_hi, mv_lo, first=True, last=True):
            nc.tensor.matmul(o, st_hi, mv_hi, start=first, stop=False)
            nc.tensor.matmul(o, st_hi, mv_lo, start=False, stop=False)
            return nc.tensor.matmul(o, st_lo, mv_hi, start=False, stop=last)

        def fillers(b, s):
            prep = {0: [("gate", 0)], 1: [("mod", 1)], 2: [("row", 0)]} if b == 0 else {}
            work = {0: [("v", 3)], 1: [("v", 4)], 2: [("v", 5)], 3: [("v", 6), ("qk", 4)], 4: [("v", 7), ("qk", 5)],
                    5: [("qk", 6)], 6: [("qk", 7)]}
            late = {5 + 2 * p: [("ctx", p)] for p in range(T // 2)}
            return work.get(s, []) + prep.get(s, []) + late.get(s, [])

        A_JOBS = [(0, "wvp", 0)]
        for b in range(B):
            A_JOBS += [(b, "v", t) for t in range(3)]
            for s in range(UNITS):
                A_JOBS += [(b, *job) for job in fillers(b, s) if job[0] != "mod"]
            A_JOBS += [(b, "pv", i) for i in range(T)] + [(b, "f2", t) for t in range(T)]
        A_READ_OUT = {"v": vlo_ready, "qk": qk32_ready, "ctx": tanh_ready, "pv": o1_ready, "f2": t2_ready,
                      "wvp": wv_lo_ready, "gate": gate_copied, "row": row_added}
        T_JOBS = []
        for b in range(B):
            if b == 0:
                T_JOBS += [(0, "mod", 0)]
            T_JOBS += [(b, "h", r) for r in range(4)]
            if b == 0:
                T_JOBS += [(0, "mod", 1)]
            T_JOBS += [(b, "p", n) for n in range(2 * UNITS)] + [(b, "h", r) for r in range(4, 8)]
        T_READ_OUT = {"h": h32_ready, "p": ptlo_ready, "mod": mod_copied}

        def a_bank(b, kind, k):
            return a_ps[A_JOBS.index((b, kind, k)) % 2]

        def t_bank(b, kind, k):
            return t_ps[T_JOBS.index((b, kind, k)) % 2]

        def read_out(jobs, signals, job):
            n = jobs.index(job)
            if n < 2:
                return None
            b, kind, k = jobs[n - 2]
            s = signals[kind]
            return s, b * per.get(s, 0) + k + 1

        def own_half(b):
            return slice(b * P // B, (b + 1) * P // B)

        def other_half(b):
            return own_half(B - 1 - b)

        def add_result(eng, e, b, t):
            wait(eng, t2_ready, b, t + 1)
            wait(eng, x2c_ready, b, t + 1)
            xt = x_all[:, b * T + t, :]
            e.tensor_tensor(xt, xt, o1[:, t % 2, :], ALU.add).then_inc(y_ready, 1)

        QK_JOBS = [(0, 0), (2, 0), (2, 1), (0, 1), (1, 0), (3, 0), (1, 1), (3, 1)]

        block = ctx.enter_context(nc.Block())

        @block.sync
        def _(sp):
            def load_x(h):
                sp.dma_start(x_all[:, h * TH:(h + 1) * TH, :], x_v[:, h * TH:(h + 1) * TH, :]).then_inc(x_in[h], 16)

            wa = w_attn.rearrange("(c p) n -> p c n", p=P)
            wm = wmod.rearrange("(c p) n -> p c n", p=P)
            sp.dma_start(cols_sb[:, :], cols).then_inc(cols_in, 16)
            load_x(0)
            sp.dma_start(wmod1_raw[:, :, :], wm[:, :, 0:2 * E]).then_inc(wmod1_in, 16)
            sp.dma_start(wattn_raw[:, :, 0:2 * E], wa[:, :, 0:2 * E]).then_inc(wqk_in, 16)
            load_x(1)
            sp.dma_start(wvt_raw[:, :, :], wv_t.rearrange("(c p) n -> p c n", p=P)).then_inc(wvt_in, 16)
            sp.dma_start(wp_raw[:, :, :], wp.rearrange("(c p) n -> p c n", p=P)).then_inc(wp_in, 16)
            sp.dma_start(wattn_raw[:, :, 2 * E:3 * E], wa[:, :, 2 * E:3 * E]).then_inc(wv_in, 16)
            sp.dma_start(wmod2_raw[:, :, :], wm[:, :, 2 * E:6 * E]).then_inc(wmod2_in, 16)
            sp.dma_start(consts[:, 0, :, :].rearrange("p v n -> p (v n)"), rows.partition_broadcast(P))\
                .then_inc(rows_in, 16)
            load_x(2)
            load_x(3)
            sp.wait_ge(gate_copied, 1)
            for b in range(B):
                sp.dma_start(gates[other_half(b), b, :, :], gates[own_half(b), b, :, :]).then_inc(gates_spread, 16)
            wait(sp, v_psum, 0, T)
            wait(sp, qk_psum, 0, 8)
            sp.dma_start(w1_raw[:, :, :], w1_t.rearrange("(c p) n -> p c n", p=P)).then_inc(w1_in, 16)
            sp.dma_start(w2_raw[:, :, :], w2_t.rearrange("(c p) n -> p c n", p=P)).then_inc(w2_in, 16)
            for b in range(B):
                for t in range(T):
                    wait(sp, y_ready, b, t + 1)
                    sp.dma_start(out_v[:, b * T + t, :], x_all[:, b * T + t, :]).then_inc(y_out, 16)
            sp.wait_ge(y_out, 16 * B * T)

        @block.gpsimd
        def _(pool):
            G = nc.gpsimd
            G.memset(ident[:, :], 0.0).then_inc(const_ready, 1)
            G.memset(minus_half[:, :], -0.5).then_inc(const_ready, 1)
            pool.wait_ge(const_ready, 2)
            G.affine_select(out=ident[:, :], in_=ident[:, :], compare_op=ALU.not_equal, fill=1.0,
                            base=0, pattern=[[-1, P]], channel_multiplier=1).then_inc(ident_ready, 1)

            def inv_std(b, n):
                h = slice((n % 2) * TH, (n % 2 + 1) * TH)
                wait(pool, ve_ready, b, n + 1)
                G.tensor_tensor(rstd[:, h], ve[:, h], minus_half[:, :], ALU.pow).then_inc(rstd_ready, 1)

            def divide_by_sum(b, u):
                wait(pool, rinv_ready, b, u + 1)
                G.tensor_scalar(prob[:, u % 3, :], prob[:, u % 3, :], rinv[:, u:u + 1], 1.0,
                                ALU.mult, ALU.mult).then_inc(pnorm_ready, 1)

            def split_ffn(n):
                src, hi, lo, arrived = (w1_raw, w1_hi, w1_lo, w1_in) if n < 4 else (w2_raw, w2_hi, w2_lo, w2_in)
                src, hi, lo = (a[:, :, :].rearrange("p c n -> p (c n)")[:, (n % 4) * HALF:(n % 4 + 1) * HALF]
                               for a in (src, hi, lo))
                pool.wait_ge(arrived, 16)
                G.tensor_scalar(hi, src, 1.0, 1.0, ALU.mult, ALU.mult).then_inc(wffn_hi, 1)
                pool.wait_ge(wffn_hi, n + 1)
                G.tensor_tensor(lo, src, f(hi), ALU.subtract).then_inc(wffn_lo, 1)

            def attn_const(b, t):
                pool.wait_ge(consts_ready, 1)
                wait(pool, xn_ready, b, 1 + t // TH)
                xt = x_all[:, b * T + t, :]
                G.tensor_tensor(xt, xt, consts[:, b, 0, :], ALU.add).then_inc(xc_ready, 1)

            def attn_residual(b, t):
                wait(pool, o1_ready, b, t + 1)
                wait(pool, xc_ready, b, t + 1)
                xt = x_all[:, b * T + t, :]
                G.tensor_tensor(xt, xt, o1[:, t % 2, :], ALU.add).then_inc(x2_ready, 1)

            def gelu_high(b, n):
                wait(pool, gelu_ready, b, n + 1)
                G.tensor_scalar(gt_hi[:, n % HC, :], f32s[:, n % 3, :], 1.0, 1.0, ALU.mult, ALU.mult)\
                    .then_inc(ghi_ready, 1)

            def ffn_const(b, t):
                wait(pool, xn_ready, b, 3 + t // TH)
                xt = x_all[:, b * T + t, :]
                G.tensor_tensor(xt, xt, consts[:, b, 1, :], ALU.add).then_inc(x2c_ready, 1)

            inv_std(0, 0)
            pool.wait_ge(wqk_hi_ready, 1)
            G.tensor_tensor(wqk_lo[:, :, :], wattn_raw[:, :, 0:2 * E], f(wqk_hi[:, :, :]), ALU.subtract)\
                .then_inc(wqk_lo_ready, 1)
            inv_std(0, 1)
            for b in range(B):
                for s in range(UNITS):
                    if s < T:
                        divide_by_sum(b, s)
                    if b == 0 and s >= T:
                        split_ffn(s - T)
                    if s >= 10:
                        attn_const(b, s - 10)
                    if s >= 11:
                        attn_residual(b, s - 11)
                attn_const(b, 6)
                inv_std(b, 2)
                attn_residual(b, 5)
                attn_const(b, 7)
                attn_residual(b, 6)
                for n in range(HC):
                    gelu_high(b, n)
                    if n == 0:
                        attn_residual(b, 7)
                    if n == 2:
                        inv_std(b, 3)
                    if n >= 4:
                        ffn_const(b, n - 4)
                for t in range(TH):
                    if b + 1 < B and t in (1, 2):
                        inv_std(b + 1, t - 1)
                    add_result(pool, G, b, t)
                for n in range(HC, 2 * HC):
                    gelu_high(b, n)
                    if n >= HC + 4:
                        ffn_const(b, n - HC)
                for t in range(TH, T if b + 1 < B else T - 1):
                    add_result(pool, G, b, t)

        @block.scalar
        def _(act):
            A = nc.scalar.activation
            act.wait_ge(cols_in, 16)
            A(exps[:, 0:EC * B], cols_sb[:, C_CT:C_CT + EC * B], ACT.Exp, scale=-1.0).then_inc(exps_ready, 1)
            act.wait_ge(lw_ready, 1)
            A(exps[:, EC * B:EC * B + 1], lw_arg[:, :], ACT.Exp, scale=-1.0).then_inc(exps_ready, 1)
            act.wait_ge(wqk_in, 16)
            A(wqk_hi[:, :, :], wattn_raw[:, :, 0:2 * E], ACT.Copy).then_inc(wqk_hi_ready, 1)

            def affine(b, r):
                wait(act, ht_psum, b, r + 1)
                if r >= 2 or b:
                    act.wait_ge(hlo_ready, b * 8 + r - 1)
                act.wait_ge(mod_ready, 1 + r // 4)
                v = 4 * (r // 4) + r % 2
                A(h32[:, r % 2, :], t_bank(b, "h", r)[:, :], ACT.Identity,
                  scale=modc[:, b, v + 2:v + 3], bias=modc[:, b, v:v + 1]).then_inc(h32_ready, 1)

            def qk_bias(b, j):
                m, h = QK_JOBS[j]
                wait(act, qk_psum, b, j + 1)
                if j >= 3:
                    wait(act, qklo_ready, b, j - 2)
                src = s_bank(j) if j < 4 else a_bank(b, "qk", j)[:, :]
                if m < 2:
                    a = A(f32s[:, j % 3, :], src, ACT.Identity, scale=QSCALE, bias=bq_scaled[:, m:m + 1])
                else:
                    a = A(f32s[:, j % 3, :], src, ACT.Identity, bias=cols_sb[:, C_BK + m - 2:C_BK + m - 1])
                a.then_inc(qk32_ready, 1)

            def v_high(b, t):
                wait(act, v_psum, b, t + 1)
                A(v_hi[:, t, :], a_bank(b, "v", t)[:, 0:NV], ACT.Copy).then_inc(vhi_ready, 1)

            def prob_high(b, u):
                for g in range(2):
                    wait(act, t_psum, b, 2 * u + g + 1)
                    if b == 0 and u == 0:
                        act.wait_ge(wv_lo_ready, 1)
                    A(pt_hi[:, (u // 2) % 2, 4 * g:4 * g + 4, (u % 2) * P:(u % 2 + 1) * P],
                      t_bank(b, "p", 2 * u + g)[:, :].rearrange("p (t n) -> p t n", n=P),
                      ACT.Copy).then_inc(pthi_ready, 1)

            def softmax_exp(b, u):
                wait(act, nmax_ready, b, u + 1)
                if u >= 3:
                    wait(act, t_psum, b, 2 * (u - 2))
                A(prob[:, u % 3, :], s_ps[u % 2][:, :], ACT.Exp, bias=nmax[:, u:u + 1],
                  accum_out=rsum[:, u:u + 1]).then_inc(exp_ready, 1)

            def cam_tanh(b, p):
                wait(act, ctx_psum, b, p + 1)
                if p >= 2:
                    wait(act, qplo_ready, b, p - 1)
                A(th[:, p % 2, :], a_bank(b, "ctx", p)[:, 0:2 * P], ACT.Tanh,
                  scale=cols_sb[:, C_GATE:C_GATE + 1], bias=gate_bias[:, :]).then_inc(tanh_ready, 1)

            def double_gates():
                act.wait_ge(gate_psum, 1)
                for g in range(B):
                    last = A(gates[own_half(g), g, :, :], a_bank(0, "gate", 0)[own_half(g), :]
                             .rearrange("p (v n) -> p v n", v=2), ACT.Copy, scale=2.0)
                last.then_inc(gate_copied, 1)

            def gelu(b, n):
                wait(act, f1_psum, b, n + 1)
                if n >= 3:
                    wait(act, glo_ready, b, n - 2)
                A(f32s[:, n % 3, :], s_bank(n % 4), ACT.Gelu,
                  bias=cols_sb[:, C_B1 + n % HC:C_B1 + n % HC + 1]).then_inc(gelu_ready, 1)

            affine(0, 0)
            affine(0, 1)
            for b in range(B):
                if b == 0:
                    act.wait_ge(wv_in, 16)
                    A(wv_hi[:, :, 0:DK], wattn_raw[:, :, 2 * E:2 * E + DK], ACT.Copy)
                    act.wait_ge(wvp_psum, 1)
                    A(wv_hi[:, :, DK:NV], a_bank(0, "wvp", 0)[:, :].rearrange("p (c n) -> p c n", c=EC), ACT.Copy)\
                        .then_inc(wv_hi_ready, 1)
                    affine(0, 2)
                    affine(0, 3)
                for j in range(4):
                    qk_bias(b, j)
                    if j >= 1:
                        v_high(b, j - 1)
                for s in range(UNITS + 2):
                    if s >= 2:
                        prob_high(b, s - 2)
                    if s < 2:
                        v_high(b, 3 + s)
                    if s < UNITS:
                        softmax_exp(b, s)
                        for kind, k in fillers(b, s):
                            if kind == "v" and s >= 2:
                                v_high(b, k)
                            if kind == "qk":
                                qk_bias(b, k)
                            if kind == "ctx":
                                cam_tanh(b, k)
                            if kind == "gate":
                                double_gates()
                affine(b, 4)
                affine(b, 5)
                for n in range(HC):
                    gelu(b, n)
                affine(b, 6)
                affine(b, 7)
                if b + 1 < B:
                    affine(b + 1, 0)
                    affine(b + 1, 1)
                for n in range(HC, 2 * HC):
                    gelu(b, n)
                if b + 1 < B:
                    affine(b + 1, 2)
                    affine(b + 1, 3)

        @block.vector
        def _(dve):
            V = nc.vector
            dve.wait_ge(cols_in, 16)
            V.tensor_scalar(lw_arg[:, :], cols_sb[:, C_W1:C_W1 + 1], DEPTH, cols_sb[:, C_W0:C_W0 + 1],
                            ALU.mult, ALU.add).then_inc(lw_ready, 1)
            V.tensor_scalar(bq_scaled[:, :], cols_sb[:, C_BQ:C_BQ + 2], QSCALE, None, ALU.mult)
            V.tensor_tensor(gate_bias[:, :], cols_sb[:, C_BVC:C_BVC + 1], cols_sb[:, C_GATE:C_GATE + 1], ALU.mult)
            V.tensor_copy(bvb[:, :, :], cols_sb[:, C_BV:C_BV + 2].rearrange("p (c a) -> p c a", a=1)
                          .to_broadcast([P, EC, P])).then_inc(bias_ready, 1)
            dve.wait_ge(exps_ready, 2)
            V.tensor_scalar(exps[:, :], exps[:, :], 1.0, None, ALU.add).then_inc(plus1_ready, 1)
            dve.wait_ge(plus1_ready, 1)
            V.reciprocal(exps[:, :], exps[:, :]).then_inc(recip_ready, 1)
            dve.wait_ge(recip_ready, 1)
            V.tensor_tensor(sct[:, :, :], cols_sb[:, C_CT:C_CT + EC * B].rearrange("p (c b) -> p c b", b=B),
                            exps[:, 0:EC * B].rearrange("p (c b) -> p c b", b=B), ALU.mult).then_inc(sct_ready, 1)
            V.tensor_scalar(lw_scaled[:, :], exps[:, EC * B:EC * B + 1], QSCALE, None, ALU.mult)
            dve.wait_ge(sct_ready, 1)
            V.tensor_copy(scb[:, :, :, :].rearrange("p c b n -> p (c b) n"),
                          sct[:, :, :].rearrange("p c b -> p (c b)").rearrange("p (m a) -> p m a", a=1)
                          .to_broadcast([P, EC * B, P // B])).then_inc(silu_ready, 1)

            def norm_stats(b, n):
                h = n % 2
                if n < 2:
                    dve.wait_ge(x_in[2 * b + h], 16)
                for t in range(h * TH, (h + 1) * TH):
                    if n >= 2:
                        wait(dve, x2_ready, b, t + 1)
                    last = V.bn_stats(bst[:, t, :], x_all[:, b * T + t, :])
                last.then_inc(bst_ready, 1)
                wait(dve, bst_ready, b, n + 1)
                for t in range(h * TH, (h + 1) * TH):
                    last = V.bn_aggr(mv[:, t, :], bst[:, t, :])
                last.then_inc(mv_ready, 1)
                wait(dve, mv_ready, b, n + 1)
                V.tensor_scalar(ve[:, h * TH:(h + 1) * TH], mv[:, h * TH:(h + 1) * TH, 1], EPS, None, ALU.add)\
                    .then_inc(ve_ready, 1)

            def norm_apply(b, n):
                h = n % 2
                wait(dve, rstd_ready, b, n + 1)
                if n or b:
                    dve.wait_ge(ht_psum, b * 8 + 2 * n)
                for t in range(TH):
                    j = h * TH + t
                    last = V.tensor_scalar(xn[:, t, :], x_all[:, b * T + j, :], mv[:, j, 0:1], rstd[:, j:j + 1],
                                           ALU.subtract, ALU.mult)
                last.then_inc(xn_ready, 1)

            def h_split(b, r):
                h, c = (r // 2) % 2, r % 2
                wait(dve, h32_ready, b, r + 1)
                if b == 0 and r == 4:
                    dve.wait_ge(wffn_lo, 8)
                dst = (slice(None), c, slice(h * HALF, (h + 1) * HALF))
                V.tensor_copy(ht_hi[dst], h32[:, r % 2, :]).then_inc(hhi_ready, 1)
                wait(dve, hhi_ready, b, r + 1)
                V.tensor_tensor(ht_lo[dst], h32[:, r % 2, :], f(ht_hi[dst]), ALU.subtract).then_inc(hlo_ready, 1)

            def qk_split(b, j):
                m, h = QK_JOBS[j]
                hi, lo = (q_hi, q_lo) if m < 2 else (k_hi, k_lo)
                dst = (slice(None), m % 2, slice(h * HALF, (h + 1) * HALF))
                wait(dve, qk32_ready, b, j + 1)
                V.tensor_copy(hi[dst], f32s[:, j % 3, :]).then_inc(qkhi_ready, 1)
                wait(dve, qkhi_ready, b, j + 1)
                V.tensor_tensor(lo[dst], f32s[:, j % 3, :], f(hi[dst]), ALU.subtract).then_inc(qklo_ready, 1)

            def v_low(b, t):
                wait(dve, vhi_ready, b, t + 1)
                V.tensor_tensor(v_lo[:, t, :], a_bank(b, "v", t)[:, 0:NV], f(v_hi[:, t, :]), ALU.subtract)\
                    .then_inc(vlo_ready, 1)

            def q_update(b, p):
                dst = (slice(None), 0, slice(2 * P * p, 2 * P * (p + 1)))
                t = th[:, p % 2, :]
                wait(dve, tanh_ready, b, p + 1)
                V.scalar_tensor_tensor(t, t, lw_scaled[:, :], f(q_lo[dst]), ALU.mult, ALU.add).then_inc(qcam_ready, 1)
                wait(dve, qcam_ready, b, 2 * p + 1)
                V.tensor_tensor(t, t, f(q_hi[dst]), ALU.add).then_inc(qcam_ready, 1)
                wait(dve, qcam_ready, b, 2 * p + 2)
                V.tensor_copy(q_hi[dst], t).then_inc(qphi_ready, 1)
                wait(dve, qphi_ready, b, p + 1)
                V.tensor_tensor(q_lo[dst], t, f(q_hi[dst]), ALU.subtract).then_inc(qplo_ready, 1)

            def prob_low(b, u):
                for g in range(2):
                    wait(dve, pthi_ready, b, 2 * u + g + 1)
                    dst = (slice(None), (u // 2) % 2, slice(4 * g, 4 * g + 4), slice((u % 2) * P, (u % 2 + 1) * P))
                    V.tensor_tensor(pt_lo[dst], t_bank(b, "p", 2 * u + g)[:, :].rearrange("p (t n) -> p t n", n=P),
                                    f(pt_hi[dst]), ALU.subtract).then_inc(ptlo_ready, 1)

            def row_max(b, u):
                wait(dve, s_psum, b, u + 1)
                V.tensor_reduce(nmax[:, u:u + 1], s_ps[u % 2][:, :], AX.X, ALU.max, negate=True).then_inc(nmax_ready, 1)

            def row_recip(b, u):
                wait(dve, exp_ready, b, u + 1)
                V.reciprocal(rinv[:, u:u + 1], rsum[:, u:u + 1]).then_inc(rinv_ready, 1)

            def attn_gated(b, i):
                wait(dve, pv_psum, b, i + 1)
                if i >= 2:
                    wait(dve, x2_ready, b, i - 1)
                elif b:
                    wait(dve, y_ready, b - 1, T - 1 + i)
                V.scalar_tensor_tensor(o1[:, i % 2, :], a_bank(b, "pv", i)[:, 0:E], rinv[:, T + i:T + i + 1],
                                       gates[:, b, 0, :], ALU.mult, ALU.mult).then_inc(o1_ready, 1)

            def ffn_gated(b, i):
                wait(dve, f2_psum, b, i + 1)
                if i >= 2:
                    wait(dve, y_ready, b, i - 1)
                else:
                    wait(dve, x2_ready, b, T - 1 + i)
                V.tensor_tensor(o1[:, i % 2, :], a_bank(b, "f2", i)[:, 0:E], gates[:, b, 1, :], ALU.mult)\
                    .then_inc(t2_ready, 1)

            def gelu_low(b, n):
                wait(dve, ghi_ready, b, n + 1)
                V.tensor_tensor(gt_lo[:, n % HC, :], f32s[:, n % 3, :], f(gt_hi[:, n % HC, :]), ALU.subtract)\
                    .then_inc(glo_ready, 1)

            def mod_columns(n):
                dve.wait_ge((mod1_psum, mod2_psum)[n], 1)
                V.tensor_copy(modc[:, :, 4 * n:4 * n + 4],
                              t_bank(0, "mod", n)[:, 0:8].rearrange("p (b v) -> p b v", b=B)).then_inc(mod_copied, 1)
                dve.wait_ge(mod_copied, n + 1)
                c = modc[:, :, 4 * n + 2:4 * n + 4]
                V.tensor_scalar(c, c, 1.0, None, ALU.add).then_inc(mod_ready, 1)

            def finish_gates():
                g2 = gates[:, :, :, :].rearrange("p b v n -> p (b v n)")
                tmp = f32s[:, 0:2, :].rearrange("p a n -> p (a n)")
                dve.wait_ge(gates_spread, 16 * B)
                V.scalar_tensor_tensor(tmp, g2, -1.0, g2, ALU.mult, ALU.max).then_inc(gate_abs, 1)
                dve.wait_ge(gate_abs, 1)
                V.tensor_scalar(g2, g2, 0.0, -0.5, ALU.is_ge, ALU.add).then_inc(gate_sign, 1)
                dve.wait_ge(gate_sign, 1)
                V.scalar_tensor_tensor(g2, tmp, 0.5, g2, ALU.max, ALU.mult).then_inc(gates_ready, 1)

            def finish_consts():
                dve.wait_ge(row_added, 1)
                dve.wait_ge(gates_ready, 1)
                V.tensor_tensor(consts[:, 1, :, :], consts[:, 0, :, :], gates[:, 1, :, :], ALU.mult).then_inc(const_other, 1)
                dve.wait_ge(const_other, 1)
                V.tensor_tensor(consts[:, 0, :, :], consts[:, 0, :, :], gates[:, 0, :, :], ALU.mult).then_inc(consts_ready, 1)

            norm_stats(0, 0)
            norm_apply(0, 0)
            mod_columns(0)
            norm_stats(0, 1)
            h_split(0, 0)
            h_split(0, 1)
            norm_apply(0, 1)
            for b in range(B):
                if b == 0:
                    dve.wait_ge(wv_hi_ready, 1)
                    V.tensor_tensor(wv_lo[:, :, 0:DK], wattn_raw[:, :, 2 * E:2 * E + DK], f(wv_hi[:, :, 0:DK]), ALU.subtract)
                    V.tensor_tensor(wv_lo[:, :, DK:NV], a_bank(0, "wvp", 0)[:, :].rearrange("p (c n) -> p c n", c=EC),
                                    f(wv_hi[:, :, DK:NV]), ALU.subtract).then_inc(wv_lo_ready, 1)
                    h_split(0, 2)
                    h_split(0, 3)
                for j in range(4):
                    qk_split(b, j)
                    if j >= 1:
                        v_low(b, j - 1)
                for s in range(UNITS + 2):
                    if s < UNITS:
                        row_max(b, s)
                    if s < 2:
                        v_low(b, 3 + s)
                    if s >= 2:
                        prob_low(b, s - 2)
                    if s < UNITS:
                        row_recip(b, s)
                    if s == UNITS:
                        norm_apply(b, 2)
                    if s >= T + 3:
                        attn_gated(b, s - T - 3)
                    if s < UNITS:
                        for kind, k in fillers(b, s):
                            if kind == "v" and s >= 2:
                                v_low(b, k)
                            if kind == "qk":
                                qk_split(b, k)
                            if kind == "ctx":
                                q_update(b, k)
                            if kind == "mod":
                                mod_columns(k)
                            if kind == "row":
                                dve.wait_ge(rows_in, 16)
                                dve.wait_ge(row_psum, 1)
                                V.tensor_tensor(consts[:, 0, 0, :], a_bank(0, "row", 0)[:, 0:E], consts[:, 0, 0, :],
                                                ALU.add).then_inc(row_added, 1)
                    if b == 0 and s == 8:
                        finish_gates()
                    if b == 0 and s == 10:
                        finish_consts()
                    if s == UNITS - 1:
                        norm_stats(b, 2)
                h_split(b, 4)
                h_split(b, 5)
                attn_gated(b, T - 1)
                for n in range(HC):
                    gelu_low(b, n)
                    if n == 0:
                        norm_stats(b, 3)
                    if n == 3:
                        norm_apply(b, 3)
                h_split(b, 6)
                h_split(b, 7)
                ffn_gated(b, 0)
                if b + 1 < B:
                    norm_stats(b + 1, 0)
                ffn_gated(b, 1)
                if b + 1 < B:
                    norm_stats(b + 1, 1)
                    norm_apply(b + 1, 0)
                for t in range(2, TH):
                    ffn_gated(b, t)
                if b + 1 < B:
                    h_split(b + 1, 0)
                    h_split(b + 1, 1)
                for n in range(HC, 2 * HC):
                    gelu_low(b, n)
                    if b + 1 < B and n == HC:
                        norm_apply(b + 1, 1)
                if b + 1 < B:
                    h_split(b + 1, 2)
                    h_split(b + 1, 3)
                for t in range(TH, T):
                    ffn_gated(b, t)
            wait(dve, y_ready, B - 1, T - 1)
            add_result(dve, V, B - 1, T - 1)

        @block.tensor
        def _(pe):
            M = nc.tensor.matmul

            def a_free(b, kind, k):
                if (w := read_out(A_JOBS, A_READ_OUT, (b, kind, k))) is not None:
                    pe.wait_ge(*w)

            def t_free(b, kind, k):
                if (w := read_out(T_JOBS, T_READ_OUT, (b, kind, k))) is not None:
                    pe.wait_ge(*w)

            def modulation(n):
                pe.wait_ge((wmod1_in, wmod2_in)[n], 16)
                pe.wait_ge(sct_ready, 1)
                t_free(0, "mod", n)
                o = t_bank(0, "mod", n)[:, 0:8].rearrange("p (b v) -> p b v", b=B)
                for v in range(4):
                    w, col = (wmod1_raw, v * P) if n == 0 else (wmod2_raw, E + v * P)
                    for k in range(EC):
                        last = M(o[:, :, v], w[:, k, col:col + P], sct[:, k, :], start=k == 0, stop=k == EC - 1)
                last.then_inc((mod1_psum, mod2_psum)[n], 1)

            def gate_rows():
                pe.wait_ge(wmod2_in, 16)
                pe.wait_ge(silu_ready, 1)
                a_free(0, "gate", 0)
                for v, col in enumerate((0, 3 * E)):
                    for k in range(EC):
                        last = M(a_bank(0, "gate", 0)[:, v * E:(v + 1) * E],
                                 scb[:, k, :, :].rearrange("p b n -> p (b n)"), wmod2_raw[:, k, col:col + E],
                                 start=k == 0, stop=k == EC - 1)
                last.then_inc(gate_psum, 1)

            def fold_projection():
                pe.wait_ge(wvt_in, 16)
                pe.wait_ge(wp_in, 16)
                o = a_bank(0, "wvp", 0)
                for m in range(EC):
                    for k in range(EC):
                        last = M(o[:, m * E:(m + 1) * E], wvt_raw[:, k, m * P:(m + 1) * P], wp_raw[:, k, :],
                                 start=k == 0, stop=k == EC - 1)
                last.then_inc(wvp_psum, 1)

            def bias_row():
                pe.wait_ge(bias_ready, 1)
                a_free(0, "row", 0)
                for k in range(EC):
                    last = M(a_bank(0, "row", 0)[:, 0:E], bvb[:, k, :], wp_raw[:, k, :], start=k == 0, stop=k == EC - 1)
                last.then_inc(row_psum, 1)

            def h_transpose(b, r):
                wait(pe, xn_ready, b, r // 2 + 1)
                t_free(b, "h", r)
                c = r % 2
                for t in range(TH):
                    last = nc.tensor.transpose(t_bank(b, "h", r)[:, t * P:(t + 1) * P], xn[:, t, c * P:(c + 1) * P],
                                               ident[:, :])
                last.then_inc(ht_psum, 1)

            def qk_project(b, j):
                m, h = QK_JOBS[j]
                if j < 4:
                    wait(pe, hlo_ready, b, 2 * h + 2)
                    if b:
                        wait(pe, gelu_ready, b - 1, 2 * HC - 3 + j)
                    o = s_bank(j)
                else:
                    a_free(b, "qk", j)
                    o = a_bank(b, "qk", j)[:, :]
                n = slice(h * HALF, (h + 1) * HALF)
                for k in range(EC):
                    last = mm3(o, wqk_hi[:, k, m * P:(m + 1) * P], wqk_lo[:, k, m * P:(m + 1) * P],
                               ht_hi[:, k, n], ht_lo[:, k, n], k == 0, k == EC - 1)
                last.then_inc(qk_psum, 1)

            def v_project(b, t):
                wait(pe, hlo_ready, b, 2 * (t // TH) + 2)
                a_free(b, "v", t)
                n = slice(t * P, (t + 1) * P)
                for k in range(EC):
                    last = mm3(a_bank(b, "v", t)[:, 0:NV], ht_hi[:, k, n], ht_lo[:, k, n], wv_hi[:, k, :],
                               wv_lo[:, k, :], k == 0, k == EC - 1)
                last.then_inc(v_psum, 1)

            def scores(b, u):
                n = slice((u % T) * P, (u % T + 1) * P)
                if u == 0:
                    wait(pe, qklo_ready, b, 3)
                if u == 2:
                    wait(pe, qklo_ready, b, 4)
                if u == 1:
                    wait(pe, qk32_ready, b, 4)
                if u >= 2:
                    wait(pe, exp_ready, b, u - 1)
                if u == T:
                    wait(pe, qklo_ready, b, 8)
                if u >= T and u % 2 == 0:
                    wait(pe, qplo_ready, b, (u - T) // 2 + 1)
                chunks = 1 if u < T else EC
                for g in range(2):
                    keys = slice(g * HALF, (g + 1) * HALF)
                    for k in range(chunks):
                        last = mm3(s_ps[u % 2][:, keys], q_hi[:, k, n], q_lo[:, k, n], k_hi[:, k, keys],
                                   k_lo[:, k, keys], k == 0, k == chunks - 1)
                last.then_inc(s_psum, 1)

            def transpose_probs(b, u):
                wait(pe, pnorm_ready if u < T else exp_ready, b, u + 1)
                for g in range(2):
                    t_free(b, "p", 2 * u + g)
                    for t in range(4):
                        c = (4 * g + t) * P
                        last = nc.tensor.transpose(t_bank(b, "p", 2 * u + g)[:, t * P:(t + 1) * P],
                                                   prob[:, u % 3, c:c + P], ident[:, :])
                    last.then_inc(t_psum, 1)

            def cam_context(b, p):
                if p == 0:
                    wait(pe, vlo_ready, b, T)
                wait(pe, ptlo_ready, b, 4 * p + 4)
                a_free(b, "ctx", p)
                for t in range(T):
                    last = mm3(a_bank(b, "ctx", p)[:, 0:2 * P], v_hi[:, t, 0:DK], v_lo[:, t, 0:DK],
                               pt_hi[:, p % 2, t, :], pt_lo[:, p % 2, t, :], t == 0, t == T - 1)
                last.then_inc(ctx_psum, 1)

            def attend(b, i):
                u = T + i
                wait(pe, ptlo_ready, b, 2 * u + 2)
                a_free(b, "pv", i)
                n = slice((u % 2) * P, (u % 2 + 1) * P)
                for t in range(T):
                    last = mm3(a_bank(b, "pv", i)[:, 0:E], pt_hi[:, (u // 2) % 2, t, n], pt_lo[:, (u // 2) % 2, t, n],
                               v_hi[:, t, DK:NV], v_lo[:, t, DK:NV], t == 0, t == T - 1)
                last.then_inc(pv_psum, 1)

            def ffn_up(b, n):
                h, c = n // HC, n % HC
                if c == 0:
                    wait(pe, hlo_ready, b, 6 + 2 * h)
                if n < 4:
                    wait(pe, exp_ready, b, UNITS - 1 + n // 2)
                else:
                    wait(pe, gelu_ready, b, n - 3)
                tokens = slice(h * HALF, (h + 1) * HALF)
                for k in range(EC):
                    last = mm3(s_bank(n % 4), w1_hi[:, k, c * P:(c + 1) * P], w1_lo[:, k, c * P:(c + 1) * P],
                               ht_hi[:, k, tokens], ht_lo[:, k, tokens], k == 0, k == EC - 1)
                last.then_inc(f1_psum, 1)

            def ffn_down(b, i):
                a_free(b, "f2", i)
                n = slice((i % TH) * P, (i % TH + 1) * P)
                for c in range(HC):
                    if i % TH == 0:
                        wait(pe, glo_ready, b, (i // TH) * HC + c + 1)
                    last = mm3(a_bank(b, "f2", i)[:, 0:E], gt_hi[:, c, n], gt_lo[:, c, n], w2_hi[:, c, :],
                               w2_lo[:, c, :], c == 0, c == HC - 1)
                last.then_inc(f2_psum, 1)

            modulation(0)
            pe.wait_ge(ident_ready, 1)
            h_transpose(0, 0)
            h_transpose(0, 1)
            fold_projection()
            pe.wait_ge(wqk_lo_ready, 1)
            qk_project(0, 0)
            h_transpose(0, 2)
            h_transpose(0, 3)
            for b in range(B):
                for j in range(1 if b == 0 else 0, 4):
                    qk_project(b, j)
                    if b == 0 and j == 1:
                        pe.wait_ge(wv_lo_ready, 1)
                    if j >= 1:
                        v_project(b, j - 1)
                for s in range(UNITS + 2):
                    if s < UNITS:
                        scores(b, s)
                    if s >= 2:
                        transpose_probs(b, s - 2)
                    if s < UNITS:
                        for kind, k in fillers(b, s):
                            if kind == "v":
                                v_project(b, k)
                            if kind == "qk":
                                qk_project(b, k)
                            if kind == "ctx":
                                cam_context(b, k)
                            if kind == "mod":
                                modulation(k)
                            if kind == "gate":
                                gate_rows()
                            if kind == "row":
                                bias_row()
                    if s >= T + 3:
                        attend(b, s - T - 3)
                h_transpose(b, 4)
                h_transpose(b, 5)
                attend(b, T - 1)
                if b == 0:
                    pe.wait_ge(wffn_lo, 8)
                for n in range(HC):
                    ffn_up(b, n)
                h_transpose(b, 6)
                h_transpose(b, 7)
                for i in range(TH):
                    ffn_down(b, i)
                if b + 1 < B:
                    h_transpose(b + 1, 0)
                    h_transpose(b + 1, 1)
                for n in range(HC, 2 * HC):
                    ffn_up(b, n)
                if b + 1 < B:
                    h_transpose(b + 1, 2)
                    h_transpose(b + 1, 3)
                for i in range(TH, T):
                    ffn_down(b, i)


def kernel(L0_attn_hidden_states, L0_attn_c_attn_w, L0_attn_c_attn_b, L0_attn_c_proj_w, L0_attn_c_proj_b,
           L0_attn_cam_gate, L0_attn_cam_w0, L0_attn_cam_w1, L0_ffn_proj1, L0_ffn_proj1_bias, L0_ffn_proj2,
           L0_ffn_proj2_bias, L0_ffn_gate_w, L0_c, L0_wmod):
    import numpy as np
    import concourse.bacc as bacc
    from concourse.bass_utils import run_bass_kernel_spmd

    def columns(v):
        return np.asarray(v).reshape(-1, P).T

    w_attn, b_attn = np.asarray(L0_attn_c_attn_w), np.asarray(L0_attn_c_attn_b)
    ct = np.asarray(L0_c).T.reshape(EC, P, B).transpose(1, 0, 2).reshape(P, EC * B)
    cols = np.concatenate([
        ct, columns(b_attn[0:E]), columns(b_attn[E:2 * E]), columns(b_attn[2 * E:2 * E + DK]), columns(b_attn[2 * E:]),
        columns(L0_attn_cam_gate), columns(L0_ffn_proj1_bias),
        np.broadcast_to(np.asarray(L0_attn_cam_w0), (P, 1)), np.broadcast_to(np.asarray(L0_attn_cam_w1), (P, 1))], axis=1)
    rows = np.concatenate([np.asarray(L0_attn_c_proj_b), np.asarray(L0_ffn_proj2_bias)]).reshape(1, 2 * E)
    arrays = {
        "x": np.asarray(L0_attn_hidden_states),
        "cols": cols,
        "wmod": np.asarray(L0_wmod),
        "w_attn": w_attn,
        "wv_t": w_attn[:, 2 * E:].T,
        "wp": np.asarray(L0_attn_c_proj_w),
        "rows": rows,
        "w1_t": np.asarray(L0_ffn_proj1).T,
        "w2_t": np.asarray(L0_ffn_proj2).T,
    }
    arrays = {n: np.ascontiguousarray(a) for n, a in arrays.items()}
    nc = bacc.Bacc("TRN2", target_bir_lowering=False, num_devices=1)
    args = [nc.dram_tensor(n, a.shape, mybir.dt.from_np(a.dtype), kind="ExternalInput").ap() for n, a in arrays.items()]
    out = nc.dram_tensor("out", (B, S, E), F32, kind="ExternalOutput").ap()
    adaln_block_kernel(nc, *args, out)
    r = run_bass_kernel_spmd(nc, [arrays], core_ids=[0])
    return r.results[0]["out"]
```
